# Optimizing a Trainium2 kernel written in Bass

```python
import numpy as np
import jax
import jax.numpy as jnp

def _softmax(x, axis=-1):
    return jax.nn.softmax(x, axis=axis)

def _gelu(x):
    return jax.nn.gelu(x, approximate=True)

def _silu(x):
    return jax.nn.silu(x)

def _sigmoid(x):
    return jax.nn.sigmoid(x)

def _layernorm(x, axis=-1, eps=1e-05):
    m = jnp.mean(x, axis=axis, keepdims=True)
    v = jnp.var(x, axis=axis, keepdims=True)
    return (x - m) / jnp.sqrt(v + eps)

def _scatter_add(tgt, idx, src, axis=0):
    return tgt.at[idx].add(src)

def _segment_sum(src, seg, n):
    return jax.ops.segment_sum(src, seg, n)
kernel_name = 'mk_xattn_seq_d4_seqx_r8_5f1086'

def setup_inputs(seed: int=0):
    np.random.seed(seed)
    _w = jnp.asarray

    def _rec_inputs():
        import jax
        import jax.numpy as jnp
        _rk = jax.random.key(seed)
        x = -0.0002928 + 1 * jax.random.normal(jax.random.fold_in(_rk, 1), (32, 64, 256), jnp.float32)
        _lenS = 64 - jax.random.randint(jax.random.fold_in(_rk, 7), (32,), 0, max(1, 64 // 4) + 1, jnp.int32)
        _lenS2 = 64 - jax.random.randint(jax.random.fold_in(_rk, 8), (32,), 0, max(1, 64 // 4) + 1, jnp.int32)
        _ctx_2048P = jax.random.normal(jax.random.fold_in(_rk, 11), (32, 16, 256), jnp.float32)
        _ctx_2048c = jax.random.dirichlet(jax.random.fold_in(_rk, 511), 0.3 * jnp.ones((16,), jnp.float32), (32, 64))
        _ctx_2048t = jnp.einsum('bsk,bkd->bsd', _ctx_2048c, _ctx_2048P)
        _ctx_2048t = _ctx_2048t * jax.lax.rsqrt(jnp.mean(jnp.square(_ctx_2048t)) + 1e-12) * 0.953939
        ctx_2048 = 0.000189249 + 0.0999589 * (_ctx_2048t + 0.3 * jax.random.normal(jax.random.fold_in(_rk, 611), (32, 64, 256), jnp.float32))
        _validS = jnp.arange(64)[None, :] < _lenS[:, None]
        _validS2 = jnp.arange(64)[None, :] < _lenS2[:, None]
        _causal = jnp.tril(jnp.ones((64, 64), dtype=bool))
        mask_BxS2_bf1 = jnp.ones((32, 64), dtype=bool)
        return (x, ctx_2048, mask_BxS2_bf1)
    x, ctx_2048, mask_BxS2_bf1 = _rec_inputs()

    def _L0_xattn_setup():
        import jax, jax.numpy as jnp
        import numpy as np
        B, L, E, H = (4, 64, 256, 32)
        S = E // H
        EXTRA_MAA, EXTRA_DECAY = (32, 64)
        EPS = 1e-05

        def _ln(x, w, b):
            m = jnp.mean(x, axis=-1, keepdims=True)
            v = jnp.mean((x - m) ** 2, axis=-1, keepdims=True)
            return (x - m) * jax.lax.rsqrt(v + EPS) * w + b

        def _token_shift(xn, prev_row):
            first = (prev_row - xn[:, 0])[:, None]
            rest = xn[:, :-1] - xn[:, 1:]
            return jnp.concatenate([first, rest], axis=1)
        key = jax.random.key(seed)
        ks = jax.random.split(key, 24)
        rn = lambda k, shp, s=1.0: jax.random.normal(k, shp, dtype=jnp.float32) * s
        return dict(x=rn(ks[0], (B, L, E)), state=rn(ks[1], (B, 2 + S, E), 0.1), ln1_w=jnp.ones((E,), jnp.float32), ln1_b=jnp.zeros((E,), jnp.float32), ln2_w=jnp.ones((E,), jnp.float32), ln2_b=jnp.zeros((E,), jnp.float32), maa_x=rn(ks[2], (E,), 0.02), maa_w1=rn(ks[3], (E, 5 * EXTRA_MAA), 0.02), maa_w2=rn(ks[4], (5, EXTRA_MAA, E), 0.02), maa_stack=rn(ks[5], (5, E), 0.02), time_decay=rn(ks[6], (E,), 0.5), decay_w1=rn(ks[7], (E, EXTRA_DECAY), 0.02), decay_w2=rn(ks[8], (EXTRA_DECAY, E), 0.02), faaaa=rn(ks[9], (H, S), 0.1), Wr=rn(ks[10], (E, E), 0.02), Wk=rn(ks[11], (E, E), 0.02), Wv=rn(ks[12], (E, E), 0.02), Wg=rn(ks[13], (E, E), 0.02), Wo=rn(ks[14], (E, E), 0.02), gn_w=jnp.ones((E,), jnp.float32), gn_b=jnp.zeros((E,), jnp.float32), ffn_maa_k=rn(ks[15], (E,), 0.02), ffn_maa_r=rn(ks[16], (E,), 0.02), ffn_Wk=rn(ks[17], (E, E), 0.02), ffn_Wr=rn(ks[18], (E, E), 0.02), ffn_Wv=rn(ks[19], (E, E), 0.02), i=0)
    _L0_xattn_all = _L0_xattn_setup()
    _L0_xattn_in = {k: v for k, v in _L0_xattn_all.items() if k in ('ln1_w', 'ln1_b', 'ln2_w', 'ln2_b', 'maa_x', 'maa_w1', 'maa_w2', 'maa_stack', 'time_decay', 'decay_w1', 'decay_w2', 'faaaa', 'Wr', 'Wk', 'Wv', 'Wg', 'Wo', 'gn_w', 'gn_b', 'ffn_maa_k', 'ffn_maa_r', 'ffn_Wk', 'ffn_Wr', 'ffn_Wv')}
    del _L0_xattn_all

    def _L1_xattn_setup():
        import jax, jax.numpy as jnp
        import numpy as np
        HIDDEN = 256
        HEADS = 16
        HEAD_DIM = HIDDEN // HEADS
        LN_EPS = 1e-05
        GATE_INIT = 0.5

        def _layer_norm(x, gamma, beta):
            mu = jnp.mean(x, axis=-1, keepdims=True)
            var = jnp.mean(jnp.square(x - mu), axis=-1, keepdims=True)
            return (x - mu) * jax.lax.rsqrt(var + LN_EPS) * gamma + beta
        key = jax.random.key(seed)
        ks = jax.random.split(key, 8)
        B, T_TEXT, T_AUDIO = (4, 256, 1500)
        s = 0.02
        return {'hidden_states': jax.random.normal(ks[0], (B, T_TEXT, HIDDEN), jnp.float32), 'audio_kv': jax.random.normal(ks[1], (B, T_AUDIO, HIDDEN), jnp.float32), 'audio_attention_mask': jnp.ones((B, T_AUDIO), dtype=bool), 'Wq': jax.random.normal(ks[2], (HIDDEN, HIDDEN), jnp.float32) * s, 'Wk': jax.random.normal(ks[3], (HIDDEN, HIDDEN), jnp.float32) * s, 'Wv': jax.random.normal(ks[4], (HIDDEN, HIDDEN), jnp.float32) * s, 'Wo': jax.random.normal(ks[5], (HIDDEN, HIDDEN), jnp.float32) * s, 'ln_gamma': jnp.ones((HIDDEN,), jnp.float32), 'ln_beta': jnp.zeros((HIDDEN,), jnp.float32), 'gate': jnp.array([GATE_INIT], jnp.float32)}
    _L1_xattn_all = _L1_xattn_setup()
    _L1_xattn_in = {k: v for k, v in _L1_xattn_all.items() if k in ('Wq', 'Wk', 'Wv', 'Wo', 'ln_gamma', 'ln_beta', 'gate')}
    del _L1_xattn_all

    def _L2_xattn_setup():
        import jax, jax.numpy as jnp
        import numpy as np
        EPS = 1e-05

        def _inorm(x):
            m = jnp.mean(x, axis=-1, keepdims=True)
            v = jnp.var(x, axis=-1, keepdims=True)
            return (x - m) * jax.lax.rsqrt(v + EPS)

        def _conv1x1(W, b, x):
            return jnp.einsum('oc,bct->bot', W, x) + b[None, :, None]
        key = jax.random.key(seed)
        ks = jax.random.split(key, 10)
        B, C, T = (4, 64, 256)
        s = 1.0 / np.sqrt(C)
        return {'x_c': jax.random.normal(ks[0], (B, C, T), jnp.float32), 'x_s': jax.random.normal(ks[1], (B, C, T), jnp.float32), 'Wn': jax.random.normal(ks[2], (C, C), jnp.float32) * s, 'bn': jax.random.normal(ks[3], (C,), jnp.float32) * s, 'Wm': jax.random.normal(ks[4], (C, C), jnp.float32) * s, 'bm': jax.random.normal(ks[5], (C,), jnp.float32) * s, 'Wl': jax.random.normal(ks[6], (C, C), jnp.float32) * s, 'bl': jax.random.normal(ks[7], (C,), jnp.float32) * s, 'Wo': jax.random.normal(ks[8], (C, C), jnp.float32) * s, 'bo': jax.random.normal(ks[9], (C,), jnp.float32) * s}
    _L2_xattn_all = _L2_xattn_setup()
    _L2_xattn_in = {k: v for k, v in _L2_xattn_all.items() if k in ('Wn', 'bn', 'Wm', 'bm', 'Wl', 'bl', 'Wo', 'bo')}
    del _L2_xattn_all

    def _L3_xattn_setup():
        import jax, jax.numpy as jnp
        import numpy as np
        B, Q, S1, S2 = (4, 32, 256, 256)
        D, H, K, F = (256, 16, 128, 1024)
        LN_EPS = 1e-05

        def _layer_norm(x, scale, offset):
            mu = jnp.mean(x, axis=-1, keepdims=True)
            var = jnp.var(x, axis=-1, keepdims=True)
            return (x - mu) * jax.lax.rsqrt(var + LN_EPS) * scale + offset

        def _cross_attention(q_in, kv_in, wq, bq, wk, bk, wv, bv, wo, bo, bias_k, bias_v):
            b, q_len, _ = q_in.shape
            t = kv_in.shape[1]
            qh = (q_in @ wq + bq).reshape(b, q_len, H, K)
            kh = (kv_in @ wk + bk).reshape(b, t, H, K)
            vh = (kv_in @ wv + bv).reshape(b, t, H, K)
            kh = jnp.concatenate([kh, jnp.broadcast_to(bias_k, (b, 1, H, K))], axis=1)
            vh = jnp.concatenate([vh, jnp.broadcast_to(bias_v, (b, 1, H, K))], axis=1)
            scale = jnp.sqrt(jnp.asarray(K, q_in.dtype))
            logits = jnp.einsum('bqhk,bthk->bhqt', qh, kh) / scale
            weights = jax.nn.softmax(logits, axis=-1)
            ctx = jnp.einsum('bhqt,bthk->bqhk', weights, vh).reshape(b, q_len, H * K)
            return ctx @ wo + bo

        def _forward(x, xf_1, xf_2, ln1_scale, ln1_offset, wq1, bq1, wk1, bk1, wv1, bv1, wo1, bo1, bias_k1, bias_v1, ln2_scale, ln2_offset, wq2, bq2, wk2, bk2, wv2, bv2, wo2, bo2, bias_k2, bias_v2, ln_mlp_scale, ln_mlp_offset, w_fc1, b_fc1, w_fc2, b_fc2):
            res = x
            h = _layer_norm(x, ln1_scale, ln1_offset)
            x = res + _cross_attention(h, xf_1, wq1, bq1, wk1, bk1, wv1, bv1, wo1, bo1, bias_k1, bias_v1)
            res = x
            h = _layer_norm(x, ln2_scale, ln2_offset)
            x = res + _cross_attention(h, xf_2, wq2, bq2, wk2, bk2, wv2, bv2, wo2, bo2, bias_k2, bias_v2)
            h = _layer_norm(x, ln_mlp_scale, ln_mlp_offset)
            h = jax.nn.gelu(h @ w_fc1 + b_fc1, approximate=False) @ w_fc2 + b_fc2
            return x + h
        key = jax.random.key(seed)
        ks = iter(jax.random.split(key, 64))

        def rn(shape, s=0.02):
            return jax.random.normal(next(ks), shape, jnp.float32) * s
        inp = {'x': rn((B, Q, D), 1.0), 'xf_1': rn((B, S1, D), 1.0), 'xf_2': rn((B, S2, D), 1.0)}
        for i in (1, 2):
            inp[f'ln{i}_scale'] = jnp.ones((D,), jnp.float32)
            inp[f'ln{i}_offset'] = jnp.zeros((D,), jnp.float32)
            inp[f'wq{i}'] = rn((D, H * K))
            inp[f'bq{i}'] = jnp.zeros((H * K,), jnp.float32)
            inp[f'wk{i}'] = rn((D, H * K))
            inp[f'bk{i}'] = jnp.zeros((H * K,), jnp.float32)
            inp[f'wv{i}'] = rn((D, H * K))
            inp[f'bv{i}'] = jnp.zeros((H * K,), jnp.float32)
            inp[f'wo{i}'] = rn((H * K, D))
            inp[f'bo{i}'] = jnp.zeros((D,), jnp.float32)
            inp[f'bias_k{i}'] = rn((1, 1, H, K))
            inp[f'bias_v{i}'] = rn((1, 1, H, K))
        inp['ln_mlp_scale'] = jnp.ones((D,), jnp.float32)
        inp['ln_mlp_offset'] = jnp.zeros((D,), jnp.float32)
        inp['w_fc1'] = rn((D, F))
        inp['b_fc1'] = jnp.zeros((F,), jnp.float32)
        inp['w_fc2'] = rn((F, D))
        inp['b_fc2'] = jnp.zeros((D,), jnp.float32)
        return inp
    _L3_xattn_all = _L3_xattn_setup()
    _L3_xattn_in = {k: v for k, v in _L3_xattn_all.items() if k in ('ln1_scale', 'ln1_offset', 'wq1', 'bq1', 'wk1', 'bk1', 'wv1', 'bv1', 'wo1', 'bo1', 'bias_k1', 'bias_v1', 'ln2_scale', 'ln2_offset', 'wq2', 'bq2', 'wk2', 'bk2', 'wv2', 'bv2', 'wo2', 'bo2', 'bias_k2', 'bias_v2', 'ln_mlp_scale', 'ln_mlp_offset', 'w_fc1', 'b_fc1', 'w_fc2', 'b_fc2')}
    del _L3_xattn_all
    return {'x': x, 'ctx_2048': ctx_2048, 'mask_BxS2_bf1': mask_BxS2_bf1, 'L0_xattn_ln1_w': _L0_xattn_in['ln1_w'], 'L0_xattn_ln1_b': _L0_xattn_in['ln1_b'], 'L0_xattn_ln2_w': _L0_xattn_in['ln2_w'], 'L0_xattn_ln2_b': _L0_xattn_in['ln2_b'], 'L0_xattn_maa_x': _L0_xattn_in['maa_x'], 'L0_xattn_maa_w1': _L0_xattn_in['maa_w1'], 'L0_xattn_maa_w2': _L0_xattn_in['maa_w2'], 'L0_xattn_maa_stack': _L0_xattn_in['maa_stack'], 'L0_xattn_time_decay': _L0_xattn_in['time_decay'], 'L0_xattn_decay_w1': _L0_xattn_in['decay_w1'], 'L0_xattn_decay_w2': _L0_xattn_in['decay_w2'], 'L0_xattn_faaaa': _L0_xattn_in['faaaa'], 'L0_xattn_Wr': _L0_xattn_in['Wr'], 'L0_xattn_Wk': _L0_xattn_in['Wk'], 'L0_xattn_Wv': _L0_xattn_in['Wv'], 'L0_xattn_Wg': _L0_xattn_in['Wg'], 'L0_xattn_Wo': _L0_xattn_in['Wo'], 'L0_xattn_gn_w': _L0_xattn_in['gn_w'], 'L0_xattn_gn_b': _L0_xattn_in['gn_b'], 'L0_xattn_ffn_maa_k': _L0_xattn_in['ffn_maa_k'], 'L0_xattn_ffn_maa_r': _L0_xattn_in['ffn_maa_r'], 'L0_xattn_ffn_Wk': _L0_xattn_in['ffn_Wk'], 'L0_xattn_ffn_Wr': _L0_xattn_in['ffn_Wr'], 'L0_xattn_ffn_Wv': _L0_xattn_in['ffn_Wv'], 'L1_xattn_Wq': _L1_xattn_in['Wq'], 'L1_xattn_Wk': _L1_xattn_in['Wk'], 'L1_xattn_Wv': _L1_xattn_in['Wv'], 'L1_xattn_Wo': _L1_xattn_in['Wo'], 'L1_xattn_ln_gamma': _L1_xattn_in['ln_gamma'], 'L1_xattn_ln_beta': _L1_xattn_in['ln_beta'], 'L1_xattn_gate': _L1_xattn_in['gate'], 'L2_xattn_Wn': _L2_xattn_in['Wn'], 'L2_xattn_bn': _L2_xattn_in['bn'], 'L2_xattn_Wm': _L2_xattn_in['Wm'], 'L2_xattn_bm': _L2_xattn_in['bm'], 'L2_xattn_Wl': _L2_xattn_in['Wl'], 'L2_xattn_bl': _L2_xattn_in['bl'], 'L2_xattn_Wo': _L2_xattn_in['Wo'], 'L2_xattn_bo': _L2_xattn_in['bo'], 'L3_xattn_ln1_scale': _L3_xattn_in['ln1_scale'], 'L3_xattn_ln1_offset': _L3_xattn_in['ln1_offset'], 'L3_xattn_wq1': _L3_xattn_in['wq1'], 'L3_xattn_bq1': _L3_xattn_in['bq1'], 'L3_xattn_wk1': _L3_xattn_in['wk1'], 'L3_xattn_bk1': _L3_xattn_in['bk1'], 'L3_xattn_wv1': _L3_xattn_in['wv1'], 'L3_xattn_bv1': _L3_xattn_in['bv1'], 'L3_xattn_wo1': _L3_xattn_in['wo1'], 'L3_xattn_bo1': _L3_xattn_in['bo1'], 'L3_xattn_bias_k1': _L3_xattn_in['bias_k1'], 'L3_xattn_bias_v1': _L3_xattn_in['bias_v1'], 'L3_xattn_ln2_scale': _L3_xattn_in['ln2_scale'], 'L3_xattn_ln2_offset': _L3_xattn_in['ln2_offset'], 'L3_xattn_wq2': _L3_xattn_in['wq2'], 'L3_xattn_bq2': _L3_xattn_in['bq2'], 'L3_xattn_wk2': _L3_xattn_in['wk2'], 'L3_xattn_bk2': _L3_xattn_in['bk2'], 'L3_xattn_wv2': _L3_xattn_in['wv2'], 'L3_xattn_bv2': _L3_xattn_in['bv2'], 'L3_xattn_wo2': _L3_xattn_in['wo2'], 'L3_xattn_bo2': _L3_xattn_in['bo2'], 'L3_xattn_bias_k2': _L3_xattn_in['bias_k2'], 'L3_xattn_bias_v2': _L3_xattn_in['bias_v2'], 'L3_xattn_ln_mlp_scale': _L3_xattn_in['ln_mlp_scale'], 'L3_xattn_ln_mlp_offset': _L3_xattn_in['ln_mlp_offset'], 'L3_xattn_w_fc1': _L3_xattn_in['w_fc1'], 'L3_xattn_b_fc1': _L3_xattn_in['b_fc1'], 'L3_xattn_w_fc2': _L3_xattn_in['w_fc2'], 'L3_xattn_b_fc2': _L3_xattn_in['b_fc2']}

def reference(x, ctx_2048, mask_BxS2_bf1, L0_xattn_ln1_w, L0_xattn_ln1_b, L0_xattn_ln2_w, L0_xattn_ln2_b, L0_xattn_maa_x, L0_xattn_maa_w1, L0_xattn_maa_w2, L0_xattn_maa_stack, L0_xattn_time_decay, L0_xattn_decay_w1, L0_xattn_decay_w2, L0_xattn_faaaa, L0_xattn_Wr, L0_xattn_Wk, L0_xattn_Wv, L0_xattn_Wg, L0_xattn_Wo, L0_xattn_gn_w, L0_xattn_gn_b, L0_xattn_ffn_maa_k, L0_xattn_ffn_maa_r, L0_xattn_ffn_Wk, L0_xattn_ffn_Wr, L0_xattn_ffn_Wv, L1_xattn_Wq, L1_xattn_Wk, L1_xattn_Wv, L1_xattn_Wo, L1_xattn_ln_gamma, L1_xattn_ln_beta, L1_xattn_gate, L2_xattn_Wn, L2_xattn_bn, L2_xattn_Wm, L2_xattn_bm, L2_xattn_Wl, L2_xattn_bl, L2_xattn_Wo, L2_xattn_bo, L3_xattn_ln1_scale, L3_xattn_ln1_offset, L3_xattn_wq1, L3_xattn_bq1, L3_xattn_wk1, L3_xattn_bk1, L3_xattn_wv1, L3_xattn_bv1, L3_xattn_wo1, L3_xattn_bo1, L3_xattn_bias_k1, L3_xattn_bias_v1, L3_xattn_ln2_scale, L3_xattn_ln2_offset, L3_xattn_wq2, L3_xattn_bq2, L3_xattn_wk2, L3_xattn_bk2, L3_xattn_wv2, L3_xattn_bv2, L3_xattn_wo2, L3_xattn_bo2, L3_xattn_bias_k2, L3_xattn_bias_v2, L3_xattn_ln_mlp_scale, L3_xattn_ln_mlp_offset, L3_xattn_w_fc1, L3_xattn_b_fc1, L3_xattn_w_fc2, L3_xattn_b_fc2):
    import jax
    import jax.numpy as jnp

    def _L0_xattn_ref(x, state, ln1_w, ln1_b, ln2_w, ln2_b, maa_x, maa_w1, maa_w2, maa_stack, time_decay, decay_w1, decay_w2, faaaa, Wr, Wk, Wv, Wg, Wo, gn_w, gn_b, ffn_maa_k, ffn_maa_r, ffn_Wk, ffn_Wr, ffn_Wv, i):
        import jax, jax.numpy as jnp
        import numpy as np
        B, L, E, H = (4, 64, 256, 32)
        S = E // H
        EXTRA_MAA, EXTRA_DECAY = (32, 64)
        EPS = 1e-05

        def _ln(x, w, b):
            m = jnp.mean(x, axis=-1, keepdims=True)
            v = jnp.mean((x - m) ** 2, axis=-1, keepdims=True)
            return (x - m) * jax.lax.rsqrt(v + EPS) * w + b

        def _token_shift(xn, prev_row):
            first = (prev_row - xn[:, 0])[:, None]
            rest = xn[:, :-1] - xn[:, 1:]
            return jnp.concatenate([first, rest], axis=1)
        b, l = (x.shape[0], x.shape[1])
        i0 = (2 + S) * i + 0
        i1 = (2 + S) * i + 1
        xn = _ln(x, ln1_w, ln1_b)
        sx = _token_shift(xn, state[:, i1])
        xxx = jnp.tanh((xn + sx * maa_x) @ maa_w1).reshape(b, l, 5, 1, EXTRA_MAA)
        xxx = jnp.matmul(xxx, maa_w2).reshape(b, l, 5, E)
        x5 = xn[:, :, None] + sx[:, :, None] * (maa_stack + xxx)
        w = jnp.exp(-jnp.exp(time_decay + jnp.tanh(x5[:, :, 1] @ decay_w1) @ decay_w2))
        w = w.reshape(b, l, H, S)
        r = (x5[:, :, 3] @ Wr.T).reshape(b, l, H, S)
        k = (x5[:, :, 0] @ Wk.T).reshape(b, l, H, S)
        v = (x5[:, :, 2] @ Wv.T).reshape(b, l, H, S)
        g = jax.nn.silu(x5[:, :, 4] @ Wg.T)
        s0 = state[:, (2 + S) * i + 2:(2 + S) * (i + 1)].reshape(b, H, S, S)
        u = faaaa[None, :, :, None]

        def step(s, rkvw):
            r_t, k_t, v_t, w_t = rkvw
            a = k_t[:, :, :, None] * v_t[:, :, None, :]
            out = jnp.einsum('bhk,bhkd->bhd', r_t, u * a + s)
            return (a + w_t[:, :, :, None] * s, out)
        xs = tuple((jnp.moveaxis(t, 1, 0) for t in (r, k, v, w)))
        _, outs = jax.lax.scan(step, s0, xs)
        att = jnp.moveaxis(outs, 0, 1).reshape(b, l, E)
        a4 = att.reshape(b, l, H, S)
        m = jnp.mean(a4, axis=-1, keepdims=True)
        var = jnp.mean((a4 - m) ** 2, axis=-1, keepdims=True)
        att = ((a4 - m) * jax.lax.rsqrt(var + EPS)).reshape(b, l, E) * gn_w + gn_b
        x = x + att * g @ Wo.T
        xn2 = _ln(x, ln2_w, ln2_b)
        sx2 = _token_shift(xn2, state[:, i0])
        xk = xn2 + sx2 * ffn_maa_k
        xr = xn2 + sx2 * ffn_maa_r
        rr = jax.nn.sigmoid(xr @ ffn_Wr.T)
        kk = jnp.square(jax.nn.relu(xk @ ffn_Wk.T))
        x = x + rr * (kk @ ffn_Wv.T)
        return x

    def _L1_xattn_ref(hidden_states, audio_kv, audio_attention_mask, Wq, Wk, Wv, Wo, ln_gamma, ln_beta, gate):
        import jax, jax.numpy as jnp
        import numpy as np
        HIDDEN = 256
        HEADS = 16
        HEAD_DIM = HIDDEN // HEADS
        LN_EPS = 1e-05
        GATE_INIT = 0.5

        def _layer_norm(x, gamma, beta):
            mu = jnp.mean(x, axis=-1, keepdims=True)
            var = jnp.mean(jnp.square(x - mu), axis=-1, keepdims=True)
            return (x - mu) * jax.lax.rsqrt(var + LN_EPS) * gamma + beta
        B, Tt, D = hidden_states.shape
        Ta = audio_kv.shape[1]
        scale = HEAD_DIM ** (-0.5)
        a = _layer_norm(audio_kv, ln_gamma, ln_beta)
        Q = (hidden_states @ Wq.T).reshape(B, Tt, HEADS, HEAD_DIM).transpose(0, 2, 1, 3)
        K = (a @ Wk.T).reshape(B, Ta, HEADS, HEAD_DIM).transpose(0, 2, 1, 3)
        V = (a @ Wv.T).reshape(B, Ta, HEADS, HEAD_DIM).transpose(0, 2, 1, 3)
        scores = jnp.einsum('bhtd,bhsd->bhts', Q, K) * scale
        mask = audio_attention_mask[:, None, None, :]
        scores = jnp.where(mask, scores, jnp.float32(-jnp.inf))
        attn = jax.nn.softmax(scores, axis=-1)
        out = jnp.einsum('bhts,bhsd->bhtd', attn, V)
        out = out.transpose(0, 2, 1, 3).reshape(B, Tt, D)
        out = out @ Wo.T
        return hidden_states + jnp.tanh(gate) * out

    def _L2_xattn_ref(x_c, x_s, Wn, bn, Wm, bm, Wl, bl, Wo, bo):
        import jax, jax.numpy as jnp
        import numpy as np
        EPS = 1e-05

        def _inorm(x):
            m = jnp.mean(x, axis=-1, keepdims=True)
            v = jnp.var(x, axis=-1, keepdims=True)
            return (x - m) * jax.lax.rsqrt(v + EPS)

        def _conv1x1(W, b, x):
            return jnp.einsum('oc,bct->bot', W, x) + b[None, :, None]
        Mn = _conv1x1(Wn, bn, _inorm(x_c))
        Mm = _conv1x1(Wm, bm, _inorm(x_s))
        A = jax.nn.softmax(jnp.einsum('bct,bcs->bts', Mn, Mm), axis=-1)
        Ml = _conv1x1(Wl, bl, x_s)
        Mo = jnp.einsum('bcs,bts->bct', Ml, A)
        return _conv1x1(Wo, bo, Mo) + x_c

    def _L3_xattn_ref(x, xf_1, xf_2, ln1_scale, ln1_offset, wq1, bq1, wk1, bk1, wv1, bv1, wo1, bo1, bias_k1, bias_v1, ln2_scale, ln2_offset, wq2, bq2, wk2, bk2, wv2, bv2, wo2, bo2, bias_k2, bias_v2, ln_mlp_scale, ln_mlp_offset, w_fc1, b_fc1, w_fc2, b_fc2):
        import jax, jax.numpy as jnp
        import numpy as np
        B, Q, S1, S2 = (4, 32, 256, 256)
        D, H, K, F = (256, 16, 128, 1024)
        LN_EPS = 1e-05

        def _layer_norm(x, scale, offset):
            mu = jnp.mean(x, axis=-1, keepdims=True)
            var = jnp.var(x, axis=-1, keepdims=True)
            return (x - mu) * jax.lax.rsqrt(var + LN_EPS) * scale + offset

        def _cross_attention(q_in, kv_in, wq, bq, wk, bk, wv, bv, wo, bo, bias_k, bias_v):
            b, q_len, _ = q_in.shape
            t = kv_in.shape[1]
            qh = (q_in @ wq + bq).reshape(b, q_len, H, K)
            kh = (kv_in @ wk + bk).reshape(b, t, H, K)
            vh = (kv_in @ wv + bv).reshape(b, t, H, K)
            kh = jnp.concatenate([kh, jnp.broadcast_to(bias_k, (b, 1, H, K))], axis=1)
            vh = jnp.concatenate([vh, jnp.broadcast_to(bias_v, (b, 1, H, K))], axis=1)
            scale = jnp.sqrt(jnp.asarray(K, q_in.dtype))
            logits = jnp.einsum('bqhk,bthk->bhqt', qh, kh) / scale
            weights = jax.nn.softmax(logits, axis=-1)
            ctx = jnp.einsum('bhqt,bthk->bqhk', weights, vh).reshape(b, q_len, H * K)
            return ctx @ wo + bo

        def _forward(x, xf_1, xf_2, ln1_scale, ln1_offset, wq1, bq1, wk1, bk1, wv1, bv1, wo1, bo1, bias_k1, bias_v1, ln2_scale, ln2_offset, wq2, bq2, wk2, bk2, wv2, bv2, wo2, bo2, bias_k2, bias_v2, ln_mlp_scale, ln_mlp_offset, w_fc1, b_fc1, w_fc2, b_fc2):
            res = x
            h = _layer_norm(x, ln1_scale, ln1_offset)
            x = res + _cross_attention(h, xf_1, wq1, bq1, wk1, bk1, wv1, bv1, wo1, bo1, bias_k1, bias_v1)
            res = x
            h = _layer_norm(x, ln2_scale, ln2_offset)
            x = res + _cross_attention(h, xf_2, wq2, bq2, wk2, bk2, wv2, bv2, wo2, bo2, bias_k2, bias_v2)
            h = _layer_norm(x, ln_mlp_scale, ln_mlp_offset)
            h = jax.nn.gelu(h @ w_fc1 + b_fc1, approximate=False) @ w_fc2 + b_fc2
            return x + h
        return _forward(x, xf_1, xf_2, ln1_scale, ln1_offset, wq1, bq1, wk1, bk1, wv1, bv1, wo1, bo1, bias_k1, bias_v1, ln2_scale, ln2_offset, wq2, bq2, wk2, bk2, wv2, bv2, wo2, bo2, bias_k2, bias_v2, ln_mlp_scale, ln_mlp_offset, w_fc1, b_fc1, w_fc2, b_fc2)
    x = _L0_xattn_ref(x, ctx_2048, L0_xattn_ln1_w, L0_xattn_ln1_b, L0_xattn_ln2_w, L0_xattn_ln2_b, L0_xattn_maa_x, L0_xattn_maa_w1, L0_xattn_maa_w2, L0_xattn_maa_stack, L0_xattn_time_decay, L0_xattn_decay_w1, L0_xattn_decay_w2, L0_xattn_faaaa, L0_xattn_Wr, L0_xattn_Wk, L0_xattn_Wv, L0_xattn_Wg, L0_xattn_Wo, L0_xattn_gn_w, L0_xattn_gn_b, L0_xattn_ffn_maa_k, L0_xattn_ffn_maa_r, L0_xattn_ffn_Wk, L0_xattn_ffn_Wr, L0_xattn_ffn_Wv, 0)
    x = _L1_xattn_ref(x, ctx_2048, mask_BxS2_bf1, L1_xattn_Wq, L1_xattn_Wk, L1_xattn_Wv, L1_xattn_Wo, L1_xattn_ln_gamma, L1_xattn_ln_beta, L1_xattn_gate)
    x = _L2_xattn_ref(x, ctx_2048, L2_xattn_Wn, L2_xattn_bn, L2_xattn_Wm, L2_xattn_bm, L2_xattn_Wl, L2_xattn_bl, L2_xattn_Wo, L2_xattn_bo)
    x = _L3_xattn_ref(x, ctx_2048, ctx_2048, L3_xattn_ln1_scale, L3_xattn_ln1_offset, L3_xattn_wq1, L3_xattn_bq1, L3_xattn_wk1, L3_xattn_bk1, L3_xattn_wv1, L3_xattn_bv1, L3_xattn_wo1, L3_xattn_bo1, L3_xattn_bias_k1, L3_xattn_bias_v1, L3_xattn_ln2_scale, L3_xattn_ln2_offset, L3_xattn_wq2, L3_xattn_bq2, L3_xattn_wk2, L3_xattn_bk2, L3_xattn_wv2, L3_xattn_bv2, L3_xattn_wo2, L3_xattn_bo2, L3_xattn_bias_k2, L3_xattn_bias_v2, L3_xattn_ln_mlp_scale, L3_xattn_ln_mlp_offset, L3_xattn_w_fc1, L3_xattn_b_fc1, L3_xattn_w_fc2, L3_xattn_b_fc2)
    return x

_drawn_inputs = setup_inputs


def setup_inputs(seed=0):
    import zlib

    import numpy as np

    out = dict(_drawn_inputs(seed))
    spreads = {'L0_xattn_ln1_w': (1.0, 0.569),
     'L0_xattn_ln1_b': (0.0, 0.572),
     'L0_xattn_ln2_w': (1.0, 0.6),
     'L0_xattn_ln2_b': (0.0, 0.8),
     'L0_xattn_gn_w': (1.0, 0.6),
     'L0_xattn_gn_b': (0.0, 0.8),
     'L1_xattn_ln_gamma': (1.0, 0.6),
     'L1_xattn_ln_beta': (0.0, 2.0),
     'L3_xattn_ln1_scale': (1.0, 0.6),
     'L3_xattn_ln1_offset': (0.0, 2.0),
     'L3_xattn_bq1': (0.0, 2.0),
     'L3_xattn_bk1': (0.0, 2.0),
     'L3_xattn_bv1': (0.0, 0.1),
     'L3_xattn_bo1': (0.0, 0.1),
     'L3_xattn_ln2_scale': (1.0, 0.6),
     'L3_xattn_ln2_offset': (0.0, 2.0),
     'L3_xattn_bq2': (0.0, 2.0),
     'L3_xattn_bk2': (0.0, 2.0),
     'L3_xattn_bv2': (0.0, 0.1),
     'L3_xattn_bo2': (0.0, 0.1),
     'L3_xattn_ln_mlp_scale': (1.0, 0.6),
     'L3_xattn_ln_mlp_offset': (0.0, 0.788),
     'L3_xattn_b_fc1': (0.0, 0.392),
     'L3_xattn_b_fc2': (0.0, 0.1)}
    factors = {'L0_xattn_maa_x': 8.0,
     'L0_xattn_maa_w1': 7.047,
     'L0_xattn_maa_w2': 7.072,
     'L0_xattn_maa_stack': 8.0,
     'L0_xattn_time_decay': 2.822,
     'L0_xattn_decay_w1': 8.0,
     'L0_xattn_decay_w2': 8.0,
     'L0_xattn_faaaa': 5.512,
     'L0_xattn_ffn_maa_k': 8.0,
     'L0_xattn_ffn_maa_r': 8.0,
     'L0_xattn_ffn_Wk': 3.08,
     'L0_xattn_ffn_Wr': 8.0,
     'L0_xattn_ffn_Wv': 2.842,
     'L1_xattn_Wq': 8.0,
     'L1_xattn_Wk': 8.0,
     'L2_xattn_bm': 64.0,
     'L3_xattn_wq1': 8.0,
     'L3_xattn_wk1': 27.657,
     'L3_xattn_wv1': 4.024,
     'L3_xattn_bias_k1': 64.0,
     'L3_xattn_bias_v1': 26.607,
     'L3_xattn_wq2': 8.0,
     'L3_xattn_wk2': 29.283,
     'L3_xattn_wv2': 4.034,
     'L3_xattn_bias_k2': 64.0,
     'L3_xattn_bias_v2': 22.957,
     'L2_xattn_bn': 3.11}
    for name, (base, spread) in spreads.items():
        noise = np.random.default_rng([zlib.crc32(name.encode()), seed]).standard_normal(out[name].shape)
        drawn = base * np.exp(spread * noise) if base else spread * noise
        out[name] = jnp.asarray(drawn.astype(out[name].dtype))
    for name, factor in factors.items():
        out[name] = (out[name] * factor).astype(out[name].dtype)
    return out
```

```python
from contextlib import ExitStack

import numpy as np

import concourse.bass as bass
from concourse import mybir

F32 = mybir.dt.float32
F32R = mybir.dt.float32r
U8 = mybir.dt.uint8
ACT = mybir.ActivationFunctionType
ALU = mybir.AluOpType
AX = mybir.AxisListType.X

P = 128
B, L, E = 32, 64, 256
C = E // P
NT = B * L // P
GB = 8
GT = GB * L
GJ = GT // P
GROUPS = B // GB
S = 8
MIX = 5
MK, MW, MV, MR, MG = range(MIX)
LORA, DLORA = 32, 64
H1 = 16
D1 = E // H1
H3 = 16
K3 = 128
F3 = 1024
FT = F3 // P
EPS = 1e-5
BANK = 512

VECS = ["ln1_w", "ln1_b", "ln2_w", "ln2_b", "maa_x", "stack0", "stack1", "stack2", "stack3", "stack4",
        "time_decay", "faaaa", "gn_w", "gn_b", "ffn_maa_k", "ffn_maa_r", "ln_gamma", "ln_beta",
        "s1", "o1", "s2", "o2", "s3", "o3"]
V0 = {n: 2 * i for i, n in enumerate(VECS)}
NV = 2 * len(VECS)
H0 = {(n, a): NV + (4 * a + m) * H3 for a in range(2) for m, n in enumerate(["bq", "bk", "bias_k", "bias_v"])}
FC0 = NV + 8 * H3
BN0 = FC0 + FT
BM0, BL0, BO0, EVEN0, GATE0 = BN0 + 1, BN0 + 2, BN0 + 3, BN0 + 4, BN0 + 6
NCOL = GATE0 + 1

SQ = ["Wr", "Wk", "Wv", "Wg", "Wo", "fWk", "fWr", "fWv", "aWq", "aWk", "aWv", "aWo"]


class Steps:

    def __init__(self, semaphore, names):
        self.sem, self.names, self.next = semaphore, names, 0

    def one(self, name):
        assert self.names[self.next % len(self.names)] == name, (name, self.names[self.next % len(self.names)])
        self.next += 1
        return 1

    def at(self, turn, name):
        return turn * len(self.names) + self.names.index(name) + 1


def program(nc, x, ctx, mask, cols, sq, maa_w1, maa_w2, dec_w1, dec_w2, sel, blocks, w2l, rows3,
            wqkv, wo3, vrows, fc1, fc2, ident, out):
    xt = x.rearrange("b l e -> (b l) e").rearrange("(j p) e -> p j e", p=P)
    ct = ctx.rearrange("b l e -> (b l) e").rearrange("(j p) e -> p j e", p=P)
    ot = out.rearrange("b l e -> (b l) e").rearrange("(j p) e -> p j e", p=P)
    s0_dram = ctx[:, 2:2 + S, :].rearrange("b r e -> b (r e)").rearrange("b (c p d) -> p c b d", c=C, p=P)
    mask_flat = mask.rearrange("b l -> (b l)")

    with ExitStack() as whole:
        def alloc(stack):
            return lambda name, shape, dt=F32: stack.enter_context(nc.sbuf_tensor(name, shape, dt))

        def sem(name):
            return whole.enter_context(nc.semaphore(name))

        keep = alloc(whole)
        ps = whole.enter_context(nc.psum_tensor("ps", [P, 8, BANK], F32))

        xres = keep("xres", [P, NT, E])
        ctx_hi = keep("ctx_hi", [P, C, B * L], F32R)
        ctx_lo = keep("ctx_lo", [P, C, B * L], F32R)
        col = keep("col", [P, NCOL])
        eye = keep("eye", [P, P])
        eps = keep("eps", [P, 1])
        brow = keep("brow", [P, 3, E])

        def vec(name, c):
            return col[:, V0[name] + c:V0[name] + c + 1]

        mixers(nc, whole, alloc, sem, ps, locals())
        attention_mlp(nc, whole, alloc, sem, ps, locals())


def mixers(nc, whole, alloc, sem, ps, k):
    xres, ctx_hi, ctx_lo, col, eye, eps, vec = (k[n] for n in ("xres", "ctx_hi", "ctx_lo", "col", "eye", "eps", "vec"))
    with ExitStack() as stack:
        sb = alloc(stack)
        wsq = sb("wsq", [P, len(SQ), C, E])
        w1m = sb("w1m", [P, C, MIX * LORA])
        w2m = sb("w2m", [P, 2, E])
        dw1 = sb("dw1", [P, C, DLORA])
        dw2 = sb("dw2", [DLORA, E])
        sel = sb("sel", [P, 2, S, P])
        blk = sb("blk", [P, 2, P])
        w2l = sb("w2l", [P, 4, P])
        s0 = sb("s0", [P, C, B, S])

        xin = sb("xin", [P, GJ, E])
        cin = sb("cin", [P, GJ, E])
        masku = sb("masku", [P, GT], U8)
        mbias = sb("mbias", [P, GT])
        st = sb("st", [P, 2 * GJ, 6])
        mv = sb("mv", [P, 2 * GJ, 2])
        sd = sb("sd", [P, 2 * GJ])
        rs = sb("rs", [P, 2 * GJ])
        xn = sb("xn", [P, GJ, E])
        cn = sb("cn", [P, GJ, E])
        ctxT = sb("ctxT", [P, C, GT])
        aT = sb("aT", [P, C, GT])
        xs = sb("xs", [P, C, GB, L + 1])
        sx = sb("sx", [P, C, GT])
        z = sb("z", [P, C, GT])
        th = sb("th", [P, C, GT])
        mix = sb("mix", [P, MIX, C * GT])
        rT = sb("rT", [P, C, GT])
        kT = sb("kT", [P, C, GT])
        vT = sb("vT", [P, C, GT])
        gT = sb("gT", [P, C, GT])
        wsh = sb("wsh", [P, C, GB, L])
        dl = sb("dl", [DLORA, GT])
        kv = sb("kv", [P, 2, GB, L])
        sc = sb("sc", [P, 2, GT])
        pr = sb("pr", [P, 2, GT])
        x1 = sb("x1", [P, GJ, E])
        veo = sb("veo", [P, 2, GJ, E])
        tg = sb("tg", [P, 1])
        red = sb("red", [P, 3, 4 * GB])
        mixT = mix[:, :, :].rearrange("p m (c t) -> p m c t", c=C)
        probs = mix[:, 0:2, :].rearrange("p m t -> p (m t)")
        probsT = mix[:, 2:4, :].rearrange("p m t -> p (m t)")

        def tok(t):
            return t[:].rearrange("p c (h e) -> p (c h) e", e=E)

        def seq(ap):
            return ap.rearrange("p (b l) -> p b l", b=GB)

        def seq3(ap):
            return ap.rearrange("p c (b l) -> p c b l", b=GB)

        def placed(ap):
            return ap.rearrange("p (q r s l) -> p q r s l", q=GB // 4, r=2, s=2)

        def by_batch(ap):
            return ap.rearrange("p (q s r l) -> p q s r l", q=GB // 4, r=2, s=2)

        def two(bank):
            return ps[:, bank:bank + 2, :]

        def tok2(bank):
            return ps[:, bank:bank + 2, :].rearrange("p c (h e) -> p (c h) e", e=E)

        loaded = sem("weights_loaded")
        x_in, c_in, m_in = sem("x_loaded"), sem("ctx_loaded"), sem("mask_loaded")
        ready = sem("constants_ready")
        free = sem("group_buffers_free")
        NCONST = 14
        HALVES = range(C)
        D = range(S)
        VB = [2, 3, 5, 6]
        PE = Steps(sem("tensor_steps"), ["ctx transposed", "a transposed", "x transposed", "lora in"]
                   + [f"lora out {n}" for n in range(2 * MIX)]
                   + ["decay in", "k", "v", "decay out", "r", "g"]
                   + [x for n in range(2 * S) for x in ([f"spread {n}"] + ([f"collect {n - 3}"] if n >= 3 else []))]
                   + [f"collect {n}" for n in range(2 * S - 3, 2 * S)]
                   + ["bonus", "mean", "var", "att out", "x1 transposed", "ffn k", "ffn r", "ffn v",
                      "x2 transposed", "k1", "v1", "q1"]
                   + [f"{s} {c}" for c in range(C) for s in ("scores", "probs transposed", "heads")]
                   + ["layer 1 out", "mm", "ml", "mn", "s2 0"]
                   + [x for j in range(GJ) for x in ([f"s2 {j + 1}"] if j + 1 < GJ else []) + [f"p2T {j}", f"mo {j}"]]
                   + ["layer 2 out"])
        AC = Steps(sem("scalar_steps"), ["sd 0", "ctxT", "aT", "xs", "th"]
                   + ["dl", "kT", "vT", "decay e", "wsh", "rT", "gate tanh"]
                   + ["gn sd", "sd 1", "xs 1", "relu", "kk", "ffn r tanh",
                      "x2T", "k1T", "veo", "q1T"]
                   + [x for c in range(C) for x in (f"exp {c}", f"probsT {c}", f"oT {c}")]
                   + ["sd 2", "mmT", "mlT", "mnT"]
                   + [x for j in range(GJ) for x in (f"exp2 {j}", f"p2T {j}")]
                   + ["moT"])
        VE = Steps(sem("vector_steps"), ["st 0", "mv 0", "rs 0", "xn", "cn", "prev", "sx", "z"]
                   + [f"mixp {n}" for n in range(2 * MIX)]
                   + ["mask m", "mask"]
                   + ["gate"]
                   + [x for n in range(2 * S) for x in (f"kv {n}", f"scan {n}")]
                   + ["ruk", "bonus v", "att", "cen", "gn rs", "gn 1", "gn 2", "y", "x1", "st 1", "mv 1", "rs 1",
                      "xn 1", "prev 1", "sx 1", "xk", "xr", "ffn m", "x2"]
                   + [f"{s} {c}" for c in range(C) for s in ("masked", "max", "less", "sum", "inv", "probs")]
                   + ["x3", "st 2", "mv 2", "rs 2", "xn 2"]
                   + [x for j in range(GJ) for x in (f"max2 {j}", f"neg2 {j}", f"inv2 {j}", f"probs2 {j}")]
                   + ["x4"])
        GP = Steps(sem("gpsimd_steps"), ["ctx hi", "ctx lo"] + [f"mix {n}" for n in range(2 * MIX)]
                   + [f"first {n}" for n in range(2)]
                   + [x for n in range(2 * S) for x in ([f"first {n + 2}"] if n + 2 < 2 * S else []) + [f"rs {n}"]]
                   + ["sq"])

        block = stack.enter_context(nc.Block())

        @block.sync
        def _(sp):
            n = 0
            for dst, src in ((col[:], k["cols"]), (eye[:], k["ident"]), (k["brow"][:], k["rows3"].partition_broadcast(P)),
                             (wsq[:], k["sq"]), (w1m[:], k["maa_w1"]), (w2m[:, 0], k["maa_w2"][0:P]),
                             (w2m[0:LORA, 1], k["maa_w2"][P:P + LORA]), (dw1[:], k["dec_w1"]),
                             (dw2[:], k["dec_w2"]), (sel[:], k["sel"]), (blk[:], k["blocks"]),
                             (w2l[:], k["w2l"])) + tuple((s0[:, c], k["s0_dram"][:, c]) for c in HALVES):
                sp.dma_start(dst, src).then_inc(loaded, 16)
                n += 1
            assert n == NCONST
            with sp.Fori(0, GROUPS) as g:
                sp.wait_ge(free, g + 1)
                sp.dma_start(xin[:], k["xt"][:, bass.ds(g * GJ, GJ), :]).then_inc(x_in, 16)
                sp.dma_start(cin[:], k["ct"][:, bass.ds(g * GJ, GJ), :]).then_inc(c_in, 16)
                sp.dma_start(masku[:], k["mask_flat"][bass.ds(g * GT, GT)].partition_broadcast(P)).then_inc(m_in, 16)

        @block.tensor
        def _(pe):
            def mm(out, lhsT, rhs, start=True, stop=True):
                return pe.matmul(out, lhsT, rhs, start=start, stop=stop)

            def turn_tiles(bank, src):
                for c in HALVES:
                    for j in range(GJ):
                        last = pe.transpose(ps[:, bank + c, j * P:(j + 1) * P], src[:, j, c * P:(c + 1) * P], eye[:])
                return last

            def to_channels(banks, w, src):
                for m in HALVES:
                    for c in HALVES:
                        last = mm(ps[:, banks[m], :], w[:, c, m * P:(m + 1) * P], src[:, c, :], c == 0, c == C - 1)
                return last

            def to_tokens(bank, w, src):
                for j in range(GJ):
                    for c in HALVES:
                        last = mm(tok2(bank)[:, j, :], src[:, c, j * P:(j + 1) * P], w[:, c, :], c == 0, c == C - 1)
                return last

            W = {n: wsq[:, i] for i, n in enumerate(SQ)}
            pe.wait_ge(loaded, 16 * NCONST)
            pe.wait_ge(ready, 1)
            with pe.Fori(0, GROUPS) as g:
                pe.wait_ge(c_in, g * 16 + 16)
                turn_tiles(0, cin).then_inc(PE.sem, PE.one("ctx transposed"))
                pe.wait_ge(VE.sem, VE.at(g, "cn"))
                turn_tiles(4, cn).then_inc(PE.sem, PE.one("a transposed"))
                turn_tiles(2, xn).then_inc(PE.sem, PE.one("x transposed"))
                pe.wait_ge(VE.sem, VE.at(g, "z"))
                for c in HALVES:
                    mm(ps[:, 6, :], w1m[:, c, 0:P], z[:, c, :], c == 0, c == 1)
                for c in HALVES:
                    last = mm(ps[0:LORA, 7, :], w1m[:, c, P:P + LORA], z[:, c, :], c == 0, c == 1)
                last.then_inc(PE.sem, PE.one("lora in"))
                pe.wait_ge(AC.sem, AC.at(g, "th"))
                for n in range(2 * MIX):
                    i, c = divmod(n, C)
                    if n >= 4:
                        pe.wait_ge(VE.sem, VE.at(g, f"mixp {n - 4}"))
                    at, part = (32 * i, 0) if i < 4 else (0, 1)
                    mm(ps[:, n % 4, :], w2m[at:at + LORA, part, c * P:(c + 1) * P],
                       th[at:at + LORA, part, :]).then_inc(PE.sem, PE.one(f"lora out {n}"))
                pe.wait_ge(GP.sem, GP.at(g, f"mix {2 * MIX - 1}"))
                for c in HALVES:
                    last = mm(ps[0:DLORA, 4, :], dw1[:, c, :], mixT[:, MW, c, :], c == 0, c == 1)
                last.then_inc(PE.sem, PE.one("decay in"))
                to_channels([0, 1], W["Wk"], mixT[:, MK]).then_inc(PE.sem, PE.one("k"))
                to_channels([2, 3], W["Wv"], mixT[:, MV]).then_inc(PE.sem, PE.one("v"))
                pe.wait_ge(AC.sem, AC.at(g, "dl"))
                for m in HALVES:
                    last = mm(ps[:, 5 + m, :], dw2[:, m * P:(m + 1) * P], dl[:])
                last.then_inc(PE.sem, PE.one("decay out"))
                to_channels([7, 4], W["Wr"], mixT[:, MR]).then_inc(PE.sem, PE.one("r"))
                pe.wait_ge(AC.sem, AC.at(g, "kT"))
                to_channels([0, 1], W["Wg"], mixT[:, MG]).then_inc(PE.sem, PE.one("g"))
                pe.wait_ge(AC.sem, AC.at(g, "rT"))

                def collect(n):
                    d, c = divmod(n, C)
                    pe.wait_ge(GP.sem, GP.at(g, f"rs {n}"))
                    mm(ps[:, [7, 4][c], :], sel[:, 1, d, :], pr[:, n % 2, :], d == 0, d == S - 1)\
                        .then_inc(PE.sem, PE.one(f"collect {n}"))

                for n in range(2 * S):
                    d, c = divmod(n, C)
                    if n >= 4:
                        pe.wait_ge(VE.sem, VE.at(g, f"kv {n - 4}"))
                    mm(ps[:, VB[n % 4], :], sel[:, 0, d, :], vT[:, c, :]).then_inc(PE.sem, PE.one(f"spread {n}"))
                    if n >= 3:
                        collect(n - 3)
                for n in range(2 * S - 3, 2 * S):
                    collect(n)
                pe.wait_ge(VE.sem, VE.at(g, "ruk"))
                for c in HALVES:
                    last = mm(ps[:, c, :], blk[:, 0, :], z[:, c, :])
                last.then_inc(PE.sem, PE.one("bonus"))
                pe.wait_ge(VE.sem, VE.at(g, "att"))
                for c in HALVES:
                    last = mm(ps[:, 2 + c, :], blk[:, 1, :], th[:, c, :])
                last.then_inc(PE.sem, PE.one("mean"))
                pe.wait_ge(GP.sem, GP.at(g, "sq"))
                for c in HALVES:
                    last = mm(ps[:, 5 + c, :], blk[:, 1, :], rT[:, c, :])
                last.then_inc(PE.sem, PE.one("var"))
                pe.wait_ge(VE.sem, VE.at(g, "y"))
                to_tokens(0, W["Wo"], z).then_inc(PE.sem, PE.one("att out"))
                pe.wait_ge(VE.sem, VE.at(g, "xn 1"))
                turn_tiles(2, xn).then_inc(PE.sem, PE.one("x1 transposed"))
                pe.wait_ge(VE.sem, VE.at(g, "xr"))
                to_channels([4, 5], W["fWk"], mixT[:, 0]).then_inc(PE.sem, PE.one("ffn k"))
                to_tokens(6, W["fWr"], mixT[:, 1]).then_inc(PE.sem, PE.one("ffn r"))
                pe.wait_ge(AC.sem, AC.at(g, "kk"))
                to_tokens(0, W["fWv"], kT).then_inc(PE.sem, PE.one("ffn v"))
                pe.wait_ge(VE.sem, VE.at(g, "x2"))
                turn_tiles(2, xin).then_inc(PE.sem, PE.one("x2 transposed"))
                to_channels([6, 7], W["aWk"], aT).then_inc(PE.sem, PE.one("k1"))
                to_tokens(0, W["aWv"], aT).then_inc(PE.sem, PE.one("v1"))
                pe.wait_ge(AC.sem, AC.at(g, "x2T"))
                to_channels([4, 5], W["aWq"], rT).then_inc(PE.sem, PE.one("q1"))
                pe.wait_ge(AC.sem, AC.at(g, "q1T"))
                for c in HALVES:
                    if c:
                        pe.wait_ge(AC.sem, AC.at(g, f"probsT {c - 1}"))
                    qe = [sc, pr][c][:].rearrange("p e t -> p (e t)")
                    for b in range(GB):
                        for r in range(4):
                            last = mm(ps[:, 2 + r, b * L:(b + 1) * L], qe[32 * r:32 * r + 32, b * P:(b + 1) * P],
                                      kT[32 * r:32 * r + 32, c, b * L:(b + 1) * L])
                    last.then_inc(PE.sem, PE.one(f"scores {c}"))
                    pe.wait_ge(VE.sem, VE.at(g, f"probs {c}"))
                    for r in range(4):
                        for j in range(GJ):
                            last = pe.transpose(ps[:, 2 + r, j * P:(j + 1) * P],
                                                probs[:, r * GT + j * P:r * GT + (j + 1) * P], eye[:])
                    last.then_inc(PE.sem, PE.one(f"probs transposed {c}"))
                    pe.wait_ge(AC.sem, AC.at(g, f"probsT {c}"))
                    pe.nop(nofuse=True)
                    for b in range(GB):
                        j, o = b // 2, L * (b % 2)
                        for r in range(4):
                            for e in range(2):
                                last = mm(ps[32 * r:32 * r + 32, 6 + b % 2, c * E + j * L:c * E + (j + 1) * L],
                                          veo[o:o + L, e, j, c * P + 32 * r:c * P + 32 * r + 32],
                                          probsT[o:o + L, r * GT + j * P + e * L:r * GT + j * P + (e + 1) * L], e == 0, e == 1)
                    last.then_inc(PE.sem, PE.one(f"heads {c}"))
                pe.wait_ge(AC.sem, AC.at(g, "oT 1"))
                to_tokens(0, W["aWo"], vT).then_inc(PE.sem, PE.one("layer 1 out"))
                for j in range(GJ):
                    last = mm(tok2(4)[:, j, :], w2l[:, 1, :], cn[:, j, :])
                last.then_inc(PE.sem, PE.one("mm"))
                for j in range(GJ):
                    for h in range(2):
                        last = mm(tok2(6)[:, j, h * P:(h + 1) * P], cin[:, j, h * P:(h + 1) * P], w2l[:, 2, :])
                last.then_inc(PE.sem, PE.one("ml"))
                pe.wait_ge(VE.sem, VE.at(g, "xn 2"))
                for j in range(GJ):
                    last = mm(tok2(2)[:, j, :], w2l[:, 0, :], xn[:, j, :])
                last.then_inc(PE.sem, PE.one("mn"))
                pe.wait_ge(AC.sem, AC.at(g, "mnT"))

                def scores2(j):
                    if j >= 2:
                        pe.wait_ge(AC.sem, AC.at(g, f"exp2 {j - 2}"))
                    for o in range(2):
                        for h in range(2):
                            last = mm(ps[:, [0, 6][j % 2] + o, h * E:(h + 1) * E], tok(rT)[o * L:o * L + L, j, h * P:(h + 1) * P],
                                      tok(kT)[o * L:o * L + L, j, :])
                    last.then_inc(PE.sem, PE.one(f"s2 {j}"))

                scores2(0)
                for j in range(GJ):
                    if j + 1 < GJ:
                        scores2(j + 1)
                    pe.wait_ge(VE.sem, VE.at(g, f"probs2 {j}"))
                    for o in range(2):
                        for h in range(2):
                            for s in range(2):
                                last = pe.transpose(ps[:, 2 + o, s * E + h * P:s * E + (h + 1) * P],
                                                    mix[:, j % 2, o * 512 + h * E + s * P:o * 512 + h * E + (s + 1) * P], eye[:])
                    last.then_inc(PE.sem, PE.one(f"p2T {j}"))
                    pe.wait_ge(AC.sem, AC.at(g, f"p2T {j}"))
                    for o in range(2):
                        for s in range(2):
                            last = mm(ps[o * L:o * L + L, 4 + j // 2, (j % 2) * E:(j % 2 + 1) * E],
                                      tok(z)[:, j, s * P + o * L:s * P + o * L + L],
                                      mix[:, 2 + j % 2, o * 512 + s * E:o * 512 + (s + 1) * E], s == 0, s == 1)
                    last.then_inc(PE.sem, PE.one(f"mo {j}"))
                pe.wait_ge(AC.sem, AC.at(g, "moT"))
                for j in range(GJ):
                    last = mm(tok2(2)[:, j, :], w2l[:, 3, :], tok(gT)[:, j, :])
                last.then_inc(PE.sem, PE.one("layer 2 out"))

        @block.scalar
        def _(act):
            def ready_by(g, producer, name):
                return producer.sem, producer.at(g, name)

            act.wait_ge(loaded, 16 * NCONST)
            act.wait_ge(ready, 1)
            act.activation(tg[:], col[:, GATE0:GATE0 + 1], ACT.Tanh).then_inc(ready, 1)
            with act.Fori(0, GROUPS) as g:
                act.wait_ge(VE.sem, VE.at(g, "mv 0"))
                act.activation(sd[:], mv[:, :, 1], ACT.Sqrt, bias=eps[:]).then_inc(AC.sem, AC.one("sd 0"))
                act.wait_ge(PE.sem, PE.at(g, "ctx transposed"))
                act.copy(ctxT[:], two(0)).then_inc(AC.sem, AC.one("ctxT"))
                act.wait_ge(PE.sem, PE.at(g, "a transposed"))
                for c in HALVES:
                    last = act.activation(aT[:, c, :], ps[:, 4 + c, :], ACT.Identity, bias=vec("ln_beta", c),
                                          scale=vec("ln_gamma", c))
                last.then_inc(AC.sem, AC.one("aT"))
                act.wait_ge(PE.sem, PE.at(g, "x transposed"))
                for c in HALVES:
                    last = act.activation(xs[:, c, :, 1:], seq(ps[:, 2 + c, :]), ACT.Identity, bias=vec("ln1_b", c),
                                          scale=vec("ln1_w", c))
                last.then_inc(AC.sem, AC.one("xs"))
                act.wait_ge(PE.sem, PE.at(g, "lora in"))
                act.activation(th[:, 0, :], ps[:, 6, :], ACT.Tanh)
                act.activation(th[0:LORA, 1, :], ps[0:LORA, 7, :], ACT.Tanh).then_inc(AC.sem, AC.one("th"))
                act.wait_ge(PE.sem, PE.at(g, "decay in"))
                act.activation(dl[:], ps[0:DLORA, 4, :], ACT.Tanh).then_inc(AC.sem, AC.one("dl"))
                act.wait_ge(PE.sem, PE.at(g, "k"))
                act.copy(kT[:], two(0)).then_inc(AC.sem, AC.one("kT"))
                act.wait_ge(PE.sem, PE.at(g, "v"))
                act.copy(vT[:], two(2)).then_inc(AC.sem, AC.one("vT"))
                act.wait_ge(PE.sem, PE.at(g, "decay out"))
                for c in HALVES:
                    last = act.activation(z[:, c, :], ps[:, 5 + c, :], ACT.Exp, bias=vec("time_decay", c))
                last.then_inc(AC.sem, AC.one("decay e"))
                act.wait_ge(AC.sem, AC.at(g, "decay e"))
                act.activation(wsh[:, :, :, 1:], seq3(z[:])[:, :, :, 0:L - 1], ACT.Exp, scale=-1.0)\
                    .then_inc(AC.sem, AC.one("wsh"))
                act.wait_ge(PE.sem, PE.at(g, "r"))
                act.copy(rT[:, 0, :], ps[:, 7, :])
                act.copy(rT[:, 1, :], ps[:, 4, :]).then_inc(AC.sem, AC.one("rT"))
                act.wait_ge(PE.sem, PE.at(g, "g"))
                act.activation(gT[:], two(0), ACT.Tanh, scale=0.5).then_inc(AC.sem, AC.one("gate tanh"))
                act.wait_ge(PE.sem, PE.at(g, "var"))
                act.activation(vT[:], two(5), ACT.Sqrt, bias=eps[:]).then_inc(AC.sem, AC.one("gn sd"))
                act.wait_ge(VE.sem, VE.at(g, "mv 1"))
                act.activation(sd[:, 0:GJ], mv[:, 0:GJ, 1], ACT.Sqrt, bias=eps[:]).then_inc(AC.sem, AC.one("sd 1"))
                act.wait_ge(PE.sem, PE.at(g, "x1 transposed"))
                for c in HALVES:
                    last = act.activation(xs[:, c, :, 1:], seq(ps[:, 2 + c, :]), ACT.Identity, bias=vec("ln2_b", c),
                                          scale=vec("ln2_w", c))
                last.then_inc(AC.sem, AC.one("xs 1"))
                act.wait_ge(PE.sem, PE.at(g, "ffn k"))
                act.activation(rT[:], two(4), ACT.Relu).then_inc(AC.sem, AC.one("relu"))
                act.wait_ge(AC.sem, AC.at(g, "relu"))
                act.activation(kT[:], rT[:], ACT.Square).then_inc(AC.sem, AC.one("kk"))
                act.wait_ge(PE.sem, PE.at(g, "ffn r"))
                act.activation(gT[:], two(6), ACT.Tanh, scale=0.5).then_inc(AC.sem, AC.one("ffn r tanh"))
                act.wait_ge(PE.sem, PE.at(g, "x2 transposed"))
                act.copy(rT[:], two(2)).then_inc(AC.sem, AC.one("x2T"))
                act.wait_ge(PE.sem, PE.at(g, "k1"))
                act.copy(kT[:], two(6)).then_inc(AC.sem, AC.one("k1T"))
                act.wait_ge(PE.sem, PE.at(g, "v1"))
                for e in range(2):
                    pick = [t.rearrange("p j (h e d) -> p j h e d", e=2, d=D1)[:, :, :, e, :] for t in (veo[:, e], tok2(0))]
                    for j in range(GJ):
                        last = act.copy(pick[0][:, j], pick[1][:, j])
                last.then_inc(AC.sem, AC.one("veo"))
                act.wait_ge(PE.sem, PE.at(g, "q1"))
                for c in HALVES:
                    for e in range(2):
                        qe = [sc, pr][c][:].rearrange("p x (b e l) -> p (x b) e l", e=2, l=L)
                        last = act.activation(qe[:, :, e, :], seq(ps[:, 4 + c, :]), ACT.Copy,
                                              scale=col[:, EVEN0 + e:EVEN0 + e + 1])
                last.then_inc(AC.sem, AC.one("q1T"))
                for c in HALVES:
                    act.wait_ge(VE.sem, VE.at(g, f"less {c}"))
                    act.activation(probs, probs, ACT.Exp).then_inc(AC.sem, AC.one(f"exp {c}"))
                    act.wait_ge(PE.sem, PE.at(g, f"probs transposed {c}"))
                    act.copy(probsT, ps[:, 2:6, :].rearrange("p r t -> p (r t)")).then_inc(AC.sem, AC.one(f"probsT {c}"))
                    act.wait_ge(PE.sem, PE.at(g, f"heads {c}"))
                    act.copy(vT[:, c, :].rearrange("p (j o l) -> p o j l", o=2, l=L),
                             ps[:, 6:8, c * E:(c + 1) * E].rearrange("p o (j l) -> p o j l", l=L)).then_inc(AC.sem, AC.one(f"oT {c}"))
                act.wait_ge(VE.sem, VE.at(g, "mv 2"))
                act.activation(sd[:, 0:GJ], mv[:, 0:GJ, 1], ACT.Sqrt, bias=eps[:]).then_inc(AC.sem, AC.one("sd 2"))
                act.wait_ge(PE.sem, PE.at(g, "mm"))
                act.activation(kT[:], two(4), ACT.Identity, bias=col[:, BM0:BM0 + 1]).then_inc(AC.sem, AC.one("mmT"))
                act.wait_ge(PE.sem, PE.at(g, "ml"))
                act.copy(z[:], two(6)).then_inc(AC.sem, AC.one("mlT"))
                act.wait_ge(PE.sem, PE.at(g, "mn"))
                act.activation(rT[:], two(2), ACT.Identity, bias=col[:, BN0:BN0 + 1]).then_inc(AC.sem, AC.one("mnT"))
                for j in range(GJ):
                    act.wait_ge(VE.sem, VE.at(g, f"neg2 {j}"))
                    for n in range(4):
                        last = act.activation(mix[:, j % 2, n * E:(n + 1) * E], ps[:, [0, 6][j % 2] + n // 2, (n % 2) * E:(n % 2 + 1) * E],
                                              ACT.Exp, bias=red[:, 0, 4 * j + n:4 * j + n + 1],
                                              accum_out=red[:, 1, 4 * j + n:4 * j + n + 1])
                    last.then_inc(AC.sem, AC.one(f"exp2 {j}"))
                    act.wait_ge(PE.sem, PE.at(g, f"p2T {j}"))
                    act.copy(mix[:, 2 + j % 2, :], two(2)).then_inc(AC.sem, AC.one(f"p2T {j}"))
                act.wait_ge(PE.sem, PE.at(g, f"mo {GJ - 1}"))
                act.activation(gT[:], two(4), ACT.Identity, bias=col[:, BL0:BL0 + 1]).then_inc(AC.sem, AC.one("moT"))

        @block.vector
        def _(ve):
            def norm_stats(n, tag, first):
                for j in range(first):
                    src = (xin[:], cin[:])[j // GJ] if tag == "0" else x1[:]
                    last = ve.bn_stats(st[:, j, :], src[:, j % GJ, :])
                last.then_inc(VE.sem, VE.one(f"st {tag}"))
                ve.drain()
                for j in range(first):
                    last = ve.bn_aggr(mv[:, j, :], st[:, j, :])
                last.then_inc(VE.sem, VE.one(f"mv {tag}"))
                ve.wait_ge(AC.sem, AC.at(n, f"sd {tag}"))
                ve.reciprocal(rs[:, 0:first], sd[:, 0:first]).then_inc(VE.sem, VE.one(f"rs {tag}"))
                ve.drain()

            def normalise(dst, src, at, name):
                for j in range(GJ):
                    last = ve.tensor_scalar(dst[:, j, :], src[:, j, :], mv[:, at + j, 0:1], rs[:, at + j:at + j + 1],
                                            ALU.subtract, ALU.mult)
                last.then_inc(VE.sem, VE.one(name))

            def shift(g, tag, row, producer):
                suffix = f" {tag}" if tag else ""
                ve.wait_ge(AC.sem, AC.at(g, "ctxT"))
                ve.tensor_copy(xs[:, :, :, 0:1], seq3(ctxT[:])[:, :, :, row:row + 1]).then_inc(VE.sem, VE.one("prev" + suffix))
                ve.drain()
                ve.wait_ge(AC.sem, AC.at(g, producer))
                ve.tensor_tensor(seq3(sx[:]), xs[:, :, :, 0:L], xs[:, :, :, 1:], ALU.subtract).then_inc(VE.sem, VE.one("sx" + suffix))
                ve.drain()

            def mixed(dst, name):
                for c in HALVES:
                    last = ve.scalar_tensor_tensor(seq(dst[:, c, :]), seq(sx[:, c, :]), vec(name, c), xs[:, c, :, 1:],
                                                   ALU.mult, ALU.add)
                return last

            ve.memset(eps[:], EPS)
            ve.memset(wsh[:], 0.0)
            ve.memset(veo[:], 0.0).then_inc(ready, 1)
            ve.wait_ge(ready, 1)
            ve.sem_inc(free, 1)
            ve.wait_ge(loaded, 16 * NCONST)
            ve.wait_ge(ready, 2)
            with ve.Fori(0, GROUPS) as g:
                ve.wait_ge(x_in, g * 16 + 16)
                ve.wait_ge(c_in, g * 16 + 16)
                norm_stats(g, "0", 2 * GJ)
                normalise(xn, xin, 0, "xn")
                normalise(cn, cin, GJ, "cn")
                shift(g, "", 1, "xs")
                mixed(z, "maa_x").then_inc(VE.sem, VE.one("z"))
                for n in range(2 * MIX):
                    i, c = divmod(n, C)
                    ve.wait_ge(PE.sem, PE.at(g, f"lora out {n}"))
                    ve.scalar_tensor_tensor(mixT[:, i, c, :], ps[:, n % 4, :], vec(f"stack{i}", c), sx[:, c, :],
                                            ALU.add, ALU.mult).then_inc(VE.sem, VE.one(f"mixp {n}"))
                ve.wait_ge(m_in, g * 16 + 16)
                ve.tensor_scalar(mbias[:], masku[:], 1.0, 3e38, ALU.subtract, ALU.mult).then_inc(VE.sem, VE.one("mask m"))
                ve.drain()
                ve.tensor_scalar(mbias[:], mbias[:], 10.0, None, ALU.mult).then_inc(VE.sem, VE.one("mask"))
                ve.wait_ge(AC.sem, AC.at(g, "gate tanh"))
                ve.scalar_tensor_tensor(gT[:], gT[:], 1.0, two(0), ALU.add, ALU.mult).then_inc(VE.sem, VE.one("gate"))
                for n in range(2 * S):
                    d, c = divmod(n, C)
                    ve.wait_ge(PE.sem, PE.at(g, f"spread {n}"))
                    if n == 0:
                        ve.wait_ge(AC.sem, AC.at(g, "rT"))
                    ve.tensor_tensor(kv[:, n % 2, :, 1:], seq(kT[:, c, :])[:, :, 0:L - 1],
                                     seq(ps[:, VB[n % 4], :])[:, :, 0:L - 1], ALU.mult).then_inc(VE.sem, VE.one(f"kv {n}"))
                    ve.drain()
                    ve.wait_ge(GP.sem, GP.at(g, f"first {n}"))
                    if n >= 2:
                        ve.wait_ge(GP.sem, GP.at(g, f"rs {n - 2}"))
                    ve.tensor_tensor_scan(sc[:, n % 2, :], wsh[:, c].rearrange("p b l -> p (b l)"),
                                          kv[:, n % 2].rearrange("p b l -> p (b l)"), 0.0, ALU.mult, ALU.add)\
                        .then_inc(VE.sem, VE.one(f"scan {n}"))
                for c in HALVES:
                    last = ve.scalar_tensor_tensor(z[:, c, :], rT[:, c, :], vec("faaaa", c), kT[:, c, :], ALU.mult, ALU.mult)
                last.then_inc(VE.sem, VE.one("ruk"))
                ve.wait_ge(PE.sem, PE.at(g, "bonus"))
                ve.tensor_tensor(sx[:], two(0), vT[:], ALU.mult).then_inc(VE.sem, VE.one("bonus v"))
                ve.drain()
                ve.wait_ge(PE.sem, PE.at(g, f"collect {2 * S - 1}"))
                ve.tensor_tensor(th[:, 0, :], ps[:, 7, :], sx[:, 0, :], ALU.add)
                ve.tensor_tensor(th[:, 1, :], ps[:, 4, :], sx[:, 1, :], ALU.add).then_inc(VE.sem, VE.one("att"))
                ve.drain()
                ve.wait_ge(PE.sem, PE.at(g, "mean"))
                ve.tensor_tensor(kT[:], th[:], two(2), ALU.subtract).then_inc(VE.sem, VE.one("cen"))
                ve.wait_ge(AC.sem, AC.at(g, "gn sd"))
                ve.reciprocal(vT[:], vT[:]).then_inc(VE.sem, VE.one("gn rs"))
                ve.drain()
                ve.tensor_tensor(vT[:], vT[:], kT[:], ALU.mult).then_inc(VE.sem, VE.one("gn 1"))
                ve.drain()
                for c in HALVES:
                    last = ve.tensor_scalar(vT[:, c, :], vT[:, c, :], vec("gn_w", c), vec("gn_b", c), ALU.mult, ALU.add)
                last.then_inc(VE.sem, VE.one("gn 2"))
                ve.drain()
                ve.scalar_tensor_tensor(z[:], vT[:], 0.5, gT[:], ALU.mult, ALU.mult).then_inc(VE.sem, VE.one("y"))
                ve.wait_ge(PE.sem, PE.at(g, "att out"))
                ve.tensor_tensor(x1[:], xin[:], tok2(0), ALU.add).then_inc(VE.sem, VE.one("x1"))
                ve.drain()
                norm_stats(g, "1", GJ)
                normalise(xn, x1, 0, "xn 1")
                shift(g, "1", 0, "xs 1")
                mixed(mixT[:, 0], "ffn_maa_k").then_inc(VE.sem, VE.one("xk"))
                mixed(mixT[:, 1], "ffn_maa_r").then_inc(VE.sem, VE.one("xr"))
                ve.wait_ge(PE.sem, PE.at(g, "ffn v"))
                ve.wait_ge(AC.sem, AC.at(g, "ffn r tanh"))
                ve.scalar_tensor_tensor(tok(vT), tok(gT), 1.0, tok2(0), ALU.add, ALU.mult).then_inc(VE.sem, VE.one("ffn m"))
                ve.drain()
                ve.scalar_tensor_tensor(xin[:], tok(vT), 0.5, x1[:], ALU.mult, ALU.add).then_inc(VE.sem, VE.one("x2"))
                rows = 4 * GB
                p3 = probs.rearrange("p (n l) -> p n l", l=L)
                for c in HALVES:
                    ve.wait_ge(PE.sem, PE.at(g, f"scores {c}"))
                    if c:
                        ve.wait_ge(PE.sem, PE.at(g, "probs transposed 0"))
                    ve.scalar_tensor_tensor(probs.rearrange("p (r t) -> p r t", r=4), ps[:, 2:6, :], float(D1) ** -0.5,
                                            mbias[:].unsqueeze(1).broadcast_to([P, 4, GT]), ALU.mult, ALU.add)\
                        .then_inc(VE.sem, VE.one(f"masked {c}"))
                    ve.drain()
                    ve.tensor_reduce(red[:, 0, :], p3, AX, ALU.max).then_inc(VE.sem, VE.one(f"max {c}"))
                    ve.drain()
                    ve.tensor_tensor(p3, p3, red[:, 0, :].unsqueeze(2).broadcast_to([P, rows, L]), ALU.subtract)\
                        .then_inc(VE.sem, VE.one(f"less {c}"))
                    ve.wait_ge(AC.sem, AC.at(g, f"exp {c}"))
                    ve.tensor_reduce(red[:, 1, :], p3, AX, ALU.add).then_inc(VE.sem, VE.one(f"sum {c}"))
                    ve.drain()
                    ve.reciprocal(red[:, 2, :], red[:, 1, :]).then_inc(VE.sem, VE.one(f"inv {c}"))
                    ve.drain()
                    ve.tensor_tensor(p3, p3, red[:, 2, :].unsqueeze(2).broadcast_to([P, rows, L]), ALU.mult)\
                        .then_inc(VE.sem, VE.one(f"probs {c}"))
                ve.wait_ge(PE.sem, PE.at(g, "layer 1 out"))
                ve.scalar_tensor_tensor(x1[:], tok2(0), tg[:], xin[:], ALU.mult, ALU.add).then_inc(VE.sem, VE.one("x3"))
                ve.drain()
                norm_stats(g, "2", GJ)
                normalise(xn, x1, 0, "xn 2")
                for j in range(GJ):
                    ve.wait_ge(PE.sem, PE.at(g, f"s2 {j}"))
                    s2 = tok2([0, 6][j % 2])
                    ve.tensor_reduce(red[:, 2, 4 * j:4 * j + 4], s2, AX, ALU.max).then_inc(VE.sem, VE.one(f"max2 {j}"))
                    ve.drain()
                    ve.tensor_scalar(red[:, 0, 4 * j:4 * j + 4], red[:, 2, 4 * j:4 * j + 4], -1.0, None, ALU.mult)\
                        .then_inc(VE.sem, VE.one(f"neg2 {j}"))
                    ve.wait_ge(AC.sem, AC.at(g, f"exp2 {j}"))
                    ve.reciprocal(red[:, 2, 4 * j:4 * j + 4], red[:, 1, 4 * j:4 * j + 4]).then_inc(VE.sem, VE.one(f"inv2 {j}"))
                    ve.drain()
                    p2 = mix[:, j % 2, :].rearrange("p (n s) -> p n s", s=E)
                    ve.tensor_tensor(p2, p2, red[:, 2, 4 * j:4 * j + 4].unsqueeze(2).broadcast_to([P, 4, E]), ALU.mult)\
                        .then_inc(VE.sem, VE.one(f"probs2 {j}"))
                ve.wait_ge(PE.sem, PE.at(g, "layer 2 out"))
                ve.scalar_tensor_tensor(xres[:, bass.ds(g * GJ, GJ), :], tok2(2), col[:, BO0:BO0 + 1], x1[:], ALU.add, ALU.add)\
                    .then_inc(VE.sem, VE.one("x4"))
                ve.drain()
                ve.sem_inc(free, 1)

        @block.gpsimd
        def _(gp):
            gp.wait_ge(loaded, 16 * NCONST)
            with gp.Fori(0, GROUPS) as g:
                gp.wait_ge(AC.sem, AC.at(g, "ctxT"))
                where = bass.ds(g * GT, GT)
                pieces = [(placed(ctx_hi[:, c, where])[:, :, :, n], placed(ctx_lo[:, c, where])[:, :, :, n],
                           by_batch(ctxT[:, c, :])[:, :, n]) for c in HALVES for n in range(2)]
                gp.nop(nofuse=True)
                for hi, lo, whole_part in pieces:
                    last = gp.tensor_copy(hi, whole_part)
                last.then_inc(GP.sem, GP.one("ctx hi"))
                gp.wait_ge(GP.sem, GP.at(g, "ctx hi"))
                for hi, lo, whole_part in pieces:
                    last = gp.tensor_tensor(lo, whole_part, hi.bitcast(F32), ALU.subtract)
                last.then_inc(GP.sem, GP.one("ctx lo"))
                for n in range(2 * MIX):
                    i, c = divmod(n, C)
                    gp.wait_ge(VE.sem, VE.at(g, f"mixp {n}"))
                    gp.tensor_tensor(seq(mixT[:, i, c, :]), seq(mixT[:, i, c, :]), xs[:, c, :, 1:], ALU.add)\
                        .then_inc(GP.sem, GP.one(f"mix {n}"))

                def first(n):
                    d, c = divmod(n, C)
                    if n >= 2:
                        gp.wait_ge(VE.sem, VE.at(g, f"scan {n - 2}"))
                        gp.nop(nofuse=True)
                    gp.tensor_copy(kv[:, n % 2, :, 0:1], s0[:, c, bass.ds(g * GB, GB), d:d + 1])\
                        .then_inc(GP.sem, GP.one(f"first {n}"))

                first(0)
                first(1)
                for n in range(2 * S):
                    d, c = divmod(n, C)
                    if n + 2 < 2 * S:
                        first(n + 2)
                    gp.wait_ge(VE.sem, VE.at(g, f"scan {n}"))
                    if n == 0:
                        gp.wait_ge(AC.sem, AC.at(g, "rT"))
                    if n >= 2:
                        gp.wait_ge(PE.sem, PE.at(g, f"collect {n - 2}"))
                    gp.tensor_tensor(pr[:, n % 2, :], rT[:, c, :], sc[:, n % 2, :], ALU.mult)\
                        .then_inc(GP.sem, GP.one(f"rs {n}"))
                gp.wait_ge(VE.sem, VE.at(g, "cen"))
                gp.tensor_tensor(rT[:], kT[:], kT[:], ALU.mult).then_inc(GP.sem, GP.one("sq"))


def attention_mlp(nc, whole, alloc, sem, ps, k):
    xres, ctx_hi, ctx_lo, col, eye, eps, brow, vec = (k[n] for n in (
        "xres", "ctx_hi", "ctx_lo", "col", "eye", "eps", "brow", "vec"))
    with ExitStack() as stack:
        sb = alloc(stack)
        h_hi = sb("h_hi", [P, C, B * L], F32R)
        h_lo = sb("h_lo", [P, C, B * L], F32R)
        xn = sb("xn3", [P, NT, E])
        tmpT = sb("tmpT", [P, 2, C, GT])
        st = sb("st3", [P, NT, 6])
        mv = sb("mv3", [P, NT, 2])
        sd = sb("sd3", [P, NT])
        rs = sb("rs3", [P, NT])
        WH = 3 * C * K3 + E
        wraw = sb("wraw", [P, 2, WH])
        w_hi = sb("w_hi", [P, 2, WH], F32R)
        w_lo = sb("w_lo", [P, 2, WH], F32R)
        vrow = sb("vrow", [P, 2, 2, K3])
        vb = sb("vb", [P, 2, K3])
        qT = sb("qT", [P, GT])
        kT = sb("k3T", [P, GB, L + 1])
        v = sb("v3", [P, 2, GJ, K3])
        e = sb("e3", [P, GJ, L + 1])
        probs = sb("probs3", [P, GJ, L])
        r3 = sb("r3", [P, 3, GJ])
        pT = sb("pT", [P, 2, P])
        c_hi = sb("c_hi", [P, GT], F32R)
        c_lo = sb("c_lo", [P, GT], F32R)
        f1raw = sb("f1raw", [P, C, F3])
        f2raw = sb("f2raw", [P, FT, E])
        f1_hi = sb("f1_hi", [P, C, F3], F32R)
        f1_lo = sb("f1_lo", [P, C, F3], F32R)
        f2_hi = sb("f2_hi", [P, FT, E], F32R)
        f2_lo = sb("f2_lo", [P, FT, E], F32R)
        hb = sb("hb", [P, 2, 4])
        ge = sb("ge", [P, 2, GT])
        g_hi = ctx_hi[:, 0, 0:2 * GT].rearrange("p (n t) -> p n t", n=2)
        g_lo = ctx_lo[:, 0, 0:2 * GT].rearrange("p (n t) -> p n t", n=2)

        ITER = H3 // 2
        SLOTS = 2 * GROUPS
        UNITS = ITER * SLOTS
        BQ, BK, BV, BS, BC0, BC1, BO = 0, 1, 2, 3, 4, 5, 6
        OWN = E
        w_loaded = [sem("w_loaded_even"), sem("w_loaded_odd")]
        s = {n: sem(n) for n in """w_ready w_used f_loaded f_ready
            q_made q_read k_made k_read v_made v_read scores_made less_made exp_made probs_made
            probs_turned pT_read ctx_made ctx_hi_made ctx_lo_made out_made out_added
            fc1_made gelu_made gelu_split fc2_made fc2_added stored""".split()}
        LP = Steps(sem("norm_tensor_steps"), [f"turned {g}" for g in range(GROUPS)])
        LA = Steps(sem("norm_scalar_steps"), ["sd"] + [f"hT {g}" for g in range(GROUPS)])
        LV = Steps(sem("norm_vector_steps"), ["mv"] + [f"xn {g}" for g in range(GROUPS)]
                   + [f"split {g}" for g in range(GROUPS)])

        def unit(att, i, j, lag=0):
            return i * SLOTS + (att * UNITS + j - lag + 1)

        def column(name, att, i, hd):
            return col[:, bass.ds(i * 2 + (H0[name, att] + hd), 1)]

        def by_half(t, h):
            return t[:].rearrange("p (q s x) -> p q s x", q=GB // 4, s=2)[:, :, h, :]

        def turns(eng, att, slots):
            slots(0, True)
            with eng.Fori(1, ITER) as i:
                slots(i, False)

        def passes(a_hi, a_lo, b_hi, b_lo):
            return ((a_hi, b_hi), (a_hi, b_lo), (a_lo, b_hi))

        block = stack.enter_context(nc.Block())

        @block.sync
        def _(sp):
            def head(par, at, first):
                if not first:
                    sp.wait_ge(s["w_ready"], at - 1)
                sp.dma_start(wraw[:, par, 0:3 * C * K3], k["wqkv"][bass.ds(at, 1)]).then_inc(w_loaded[par], 16)
                sp.dma_start(wraw[:, par, 3 * C * K3:], k["wo3"][bass.ds(at, 1)]).then_inc(w_loaded[par], 16)
                sp.dma_start(vrow[:, par], k["vrows"][bass.ds(at, 1)].partition_broadcast(P)).then_inc(w_loaded[par], 16)

            head(0, 0, True)
            sp.dma_start(f1raw[:], k["fc1"]).then_inc(s["f_loaded"], 16)
            sp.dma_start(f2raw[:], k["fc2"]).then_inc(s["f_loaded"], 16)
            head(1, 1, True)
            with sp.Fori(1, H3) as i:
                for par in range(2):
                    head(par, i * 2 + par, False)
            for g in range(GROUPS):
                sp.wait_ge(s["fc2_added"], g + 1)
                sp.dma_start(k["ot"][:, g * GJ:(g + 1) * GJ, :], xres[:, g * GJ:(g + 1) * GJ, :]).then_inc(s["stored"], 16)
            sp.wait_ge(s["stored"], 16 * GROUPS)

        @block.gpsimd
        def _(gp):
            def head(par, n, i, first):
                gp.wait_ge(w_loaded[par], i * 48 + 48)
                if not first:
                    gp.wait_ge(s["w_used"], n - 1)
                gp.nop(nofuse=True)
                gp.tensor_copy(w_hi[:, par, :], wraw[:, par, :])
                gp.tensor_tensor(vb[:, par, :], vrow[:, par, 0, :], vrow[:, par, 1, :], ALU.subtract)
                gp.drain()
                gp.tensor_tensor(w_lo[:, par, :], wraw[:, par, :], w_hi[:, par, :].bitcast(F32), ALU.subtract)\
                    .then_inc(s["w_ready"], 1)

            head(0, 0, 0, True)
            head(1, 1, 0, True)
            with gp.Fori(1, H3) as i:
                for par in range(2):
                    head(par, i * 2 + par, i, False)
            gp.wait_ge(s["f_loaded"], 32)
            gp.tensor_copy(f1_hi[:], f1raw[:])
            gp.tensor_copy(f2_hi[:], f2raw[:])
            gp.drain()
            gp.tensor_tensor(f1_lo[:], f1raw[:], f1_hi[:].bitcast(F32), ALU.subtract)
            gp.tensor_tensor(f2_lo[:], f2raw[:], f2_hi[:].bitcast(F32), ALU.subtract).then_inc(s["f_ready"], 1)

        @block.tensor
        def _(pe):
            def products(out, terms, halves):
                every = [(a(c), b(c)) for c in range(halves) for a, b in terms]
                for n, (a, b) in enumerate(every):
                    last = pe.matmul(out, a, b, start=n == 0, stop=n == len(every) - 1)
                return last

            def norm(t):
                for g in range(GROUPS):
                    pe.wait_ge(LV.sem, LV.at(t, f"xn {g}"))
                    if g >= 2:
                        pe.wait_ge(LA.sem, LA.at(t, f"hT {g - 2}"))
                    for c in range(C):
                        for j in range(GJ):
                            last = pe.transpose(ps[:, 2 * (g % 2) + c, j * P:(j + 1) * P],
                                                xn[:, g * GJ + j, c * P:(c + 1) * P], eye[:])
                    last.then_inc(LP.sem, LP.one(f"turned {g}"))

            def attention(att):
                def weights(part, par, m):
                    return lambda c: part[:, par, (m * C + c) * K3:(m * C + c + 1) * K3]

                def acts(part, g, width=GT, at=0):
                    return lambda c: part[:, c, g * GT + at:g * GT + at + width]

                def turn_probs(i, j, first):
                    pe.wait_ge(s["probs_made"], unit(att, i, j))
                    if not first:
                        pe.wait_ge(s["pT_read"], unit(att, i, j, 1))
                    for p in range(2):
                        last = pe.transpose(ps[:, BC0, OWN + p * P:OWN + (p + 1) * P], probs[:, 2 * p:2 * p + 2, :], eye[:])
                    last.then_inc(s["probs_turned"], 1)

                def heads_out(i, j, first):
                    par = j % 2
                    pe.wait_ge(s["pT_read"], unit(att, i, j))
                    pe.wait_ge(s["v_read"], unit(att, i, j))
                    if not first:
                        pe.wait_ge(s["ctx_lo_made"], unit(att, i, j, 1))
                    for p in range(2):
                        for r in range(2):
                            for h in range(2):
                                last = pe.matmul(ps[:, [BC0, BC1][h], p * P + r * L:p * P + (r + 1) * L],
                                                 v[h * L:(h + 1) * L, par, 2 * p + r, :],
                                                 pT[h * L:(h + 1) * L, p, r * L:(r + 1) * L], start=True, stop=True)
                    last.then_inc(s["ctx_made"], 1)

                def project_out(i, j, first):
                    par = (j // GROUPS) % 2
                    pe.wait_ge(s["ctx_lo_made"], unit(att, i, j))
                    if not first:
                        pe.wait_ge(s["out_added"], unit(att, i, j, 1))
                    for t in range(GJ):
                        terms = [(lambda c, a=a, t=t: a[:, t * P:(t + 1) * P], lambda c, b=b: b[:, par, 3 * C * K3:])
                                 for a, b in passes(c_hi, c_lo, w_hi, w_lo)]
                        last = products(ps[:, BO + t // 2, (t % 2) * E:(t % 2 + 1) * E], terms, 1)
                    last.then_inc(s["out_made"], 1)
                    if j % GROUPS == GROUPS - 1:
                        pe.drain()
                        pe.sem_inc(s["w_used"], 1)

                def slots(i, peeled):
                    for j in range(SLOTS):
                        hd, g = divmod(j, GROUPS)
                        first = peeled and j == 0
                        second = peeled and j == 1
                        if g == 0:
                            pe.wait_ge(s["w_ready"], i * 2 + (att * H3 + hd + 1))
                        if not first:
                            pe.wait_ge(s["q_read"], unit(att, i, j, 1))
                        elif att:
                            pe.wait_ge(s["q_read"], att * UNITS)
                        products(ps[:, BQ, :], [(weights(a, hd, 0), acts(b, g)) for a, b in passes(w_hi, w_lo, h_hi, h_lo)], C)\
                            .then_inc(s["q_made"], 1)
                        if not first:
                            pe.wait_ge(s["k_read"], unit(att, i, j, 1))
                        products(ps[:, BK, :], [(weights(a, hd, 1), acts(b, g)) for a, b in passes(w_hi, w_lo, ctx_hi, ctx_lo)], C)\
                            .then_inc(s["k_made"], 1)
                        if not first:
                            turn_probs(i, j - 1, second)
                            pe.wait_ge(s["v_read"], unit(att, i, j, 1))
                        for t in range(GJ):
                            last = products(ps[:, BV, t * K3:(t + 1) * K3],
                                            [(acts(a, g, P, t * P), weights(b, hd, 2)) for a, b in passes(ctx_hi, ctx_lo, w_hi, w_lo)], C)
                        last.then_inc(s["v_made"], 1)
                        if not first:
                            heads_out(i, j - 1, second)
                        pe.wait_ge(s["q_read"], unit(att, i, j))
                        pe.wait_ge(s["k_read"], unit(att, i, j))
                        if not first:
                            pe.wait_ge(s["less_made"], unit(att, i, j, 1))
                        for b in range(GB):
                            place = b // 4 * 4 + b % 2 * 2 + b // 2 % 2
                            last = pe.matmul(ps[b % 2 * L:b % 2 * L + L, BS, b // 2 * (L + 1):(b // 2 + 1) * (L + 1)],
                                             qT[:, b * L:(b + 1) * L], kT[:, place, :], start=True, stop=True)
                        last.then_inc(s["scores_made"], 1)
                        if not first:
                            project_out(i, j - 1, second)

                turns(pe, att, slots)
                i, j = ITER - 1, SLOTS - 1
                turn_probs(i, j, False)
                heads_out(i, j, False)
                project_out(i, j, False)

            for att in range(2):
                norm(att)
                pe.wait_ge(LV.sem, LV.at(att, f"split {GROUPS - 1}"))
                attention(att)
            norm(2)
            pe.wait_ge(LV.sem, LV.at(2, f"split {GROUPS - 1}"))
            pe.wait_ge(s["f_ready"], 1)
            for g in range(GROUPS):
                for n in range(FT + 1):
                    m = g * FT + n
                    if n < FT:
                        if m >= 2:
                            pe.wait_ge(s["gelu_made"], m - 1)
                        terms = [(lambda c, a=a: a[:, c, n * P:(n + 1) * P], lambda c, b=b: b[:, c, g * GT:(g + 1) * GT])
                                 for a, b in passes(f1_hi, f1_lo, h_hi, h_lo)]
                        products(ps[:, n % 2, :], terms, C).then_inc(s["fc1_made"], 1)
                    if n:
                        f = n - 1
                        pe.wait_ge(s["gelu_split"], g * FT + f + 1)
                        if f == 0 and g:
                            pe.wait_ge(s["fc2_added"], g)
                        for t in range(GJ):
                            three = passes(g_hi, g_lo, f2_hi, f2_lo)
                            for o, (a, b) in enumerate(three):
                                last = pe.matmul(ps[:, 4 + t, 0:E], a[:, f % 2, t * P:(t + 1) * P], b[:, f, :],
                                                 start=f == 0 and o == 0, stop=f == FT - 1 and o == 2)
                        last.then_inc(s["fc2_made"], 1)

        @block.scalar
        def _(act):
            def norm(t):
                act.wait_ge(LV.sem, LV.at(t, "mv"))
                act.activation(sd[:], mv[:, :, 1], ACT.Sqrt, bias=eps[:]).then_inc(LA.sem, LA.one("sd"))
                for g in range(GROUPS):
                    act.wait_ge(LP.sem, LP.at(t, f"turned {g}"))
                    if g >= 2:
                        act.wait_ge(LV.sem, LV.at(t, f"split {g - 2}"))
                    for c in range(C):
                        last = act.activation(tmpT[:, g % 2, c, :], ps[:, 2 * (g % 2) + c, :], ACT.Identity,
                                              bias=vec(f"o{t + 1}", c), scale=vec(f"s{t + 1}", c))
                    last.then_inc(LA.sem, LA.one(f"hT {g}"))

            def attention(att):
                def probs_out(i, j):
                    act.wait_ge(s["probs_turned"], unit(att, i, j))
                    act.copy(pT[:], ps[:, BC0, OWN:OWN + 2 * P].rearrange("p (n q) -> p n q", n=2)).then_inc(s["pT_read"], 1)

                def ctx_out(i, j):
                    act.wait_ge(s["ctx_made"], unit(att, i, j))
                    for h in range(2):
                        last = act.activation(by_half(c_hi, h), ps[:, BC0 + h, 0:2 * P].rearrange("p (q x) -> p q x", q=2),
                                              ACT.Identity, bias=hb[:, j // GROUPS % 2, 3:4])
                    last.then_inc(s["ctx_hi_made"], 1)

                def slots(i, peeled):
                    for j in range(SLOTS):
                        hd, g = divmod(j, GROUPS)
                        first = peeled and j == 0
                        if g == 0:
                            for m, name in enumerate(("bq", "bk", "bias_k")):
                                act.copy(hb[:, hd, m:m + 1], column(name, att, i, hd))
                            act.copy(hb[:, hd, 3:4], column("bias_v", att, i, hd))
                            act.drain()
                        act.wait_ge(s["q_made"], unit(att, i, j))
                        act.activation(qT[:], ps[:, BQ, :], ACT.Identity, bias=hb[:, hd, 0:1]).then_inc(s["q_read"], 1)
                        act.wait_ge(s["k_made"], unit(att, i, j))
                        if g == 0:
                            act.copy(kT[:, :, L:L + 1], hb[:, hd, 2:3].unsqueeze(1).broadcast_to([P, GB, 1]))
                        act.activation(kT[:, :, 0:L], ps[:, BK, :].rearrange("p (b l) -> p b l", b=GB), ACT.Identity,
                                       bias=hb[:, hd, 1:2]).then_inc(s["k_read"], 1)
                        if not first:
                            probs_out(i, j - 1)
                            ctx_out(i, j - 1)
                        act.wait_ge(s["less_made"], unit(att, i, j))
                        act.activation(e[:], e[:], ACT.Exp, scale=float(K3) ** -0.5).then_inc(s["exp_made"], 1)

                turns(act, att, slots)
                probs_out(ITER - 1, SLOTS - 1)
                ctx_out(ITER - 1, SLOTS - 1)

            for att in range(2):
                norm(att)
                attention(att)
            norm(2)
            for m in range(GROUPS * FT):
                act.wait_ge(s["fc1_made"], m + 1)
                if m >= 2:
                    act.wait_ge(s["gelu_split"], m - 1)
                act.activation(ge[:, m % 2, :], ps[:, m % 2, :], ACT.Gelu, bias=col[:, FC0 + m % FT:FC0 + m % FT + 1])\
                    .then_inc(s["gelu_made"], 1)

        @block.vector
        def _(ve):
            def norm(t):
                for j in range(NT):
                    ve.bn_stats(st[:, j, :], xres[:, j, :])
                ve.drain()
                for j in range(NT):
                    last = ve.bn_aggr(mv[:, j, :], st[:, j, :])
                last.then_inc(LV.sem, LV.one("mv"))
                ve.wait_ge(LA.sem, LA.at(t, "sd"))
                ve.reciprocal(rs[:], sd[:])
                ve.drain()
                for g in range(GROUPS):
                    for j in range(g * GJ, (g + 1) * GJ):
                        last = ve.tensor_scalar(xn[:, j, :], xres[:, j, :], mv[:, j, 0:1], rs[:, j:j + 1], ALU.subtract, ALU.mult)
                    last.then_inc(LV.sem, LV.one(f"xn {g}"))
                ve.drain()
                for g in range(GROUPS):
                    tiles = xres[:, g * GJ:(g + 1) * GJ, :]
                    ve.tensor_tensor(tiles, tiles, brow[:, t:t + 1, :].broadcast_to([P, GJ, E]), ALU.add)
                    ve.wait_ge(LA.sem, LA.at(t, f"hT {g}"))
                    where = slice(g * GT, (g + 1) * GT)
                    ve.tensor_copy(h_hi[:, :, where], tmpT[:, g % 2])
                    ve.drain()
                    ve.tensor_tensor(h_lo[:, :, where], tmpT[:, g % 2], h_hi[:, :, where].bitcast(F32), ALU.subtract)\
                        .then_inc(LV.sem, LV.one(f"split {g}"))

            def attention(att):
                def ctx_lo_part(i, j):
                    ve.wait_ge(s["ctx_hi_made"], unit(att, i, j))
                    for h in range(2):
                        last = ve.scalar_tensor_tensor(by_half(c_lo, h), ps[:, BC0 + h, 0:2 * P].rearrange("p (q x) -> p q x", q=2),
                                                       hb[:, j // GROUPS % 2, 3:4], by_half(c_hi, h).bitcast(F32), ALU.add, ALU.subtract)
                    last.then_inc(s["ctx_lo_made"], 1)

                def add_out(i, j):
                    g = j % GROUPS
                    ve.wait_ge(s["out_made"], unit(att, i, j))
                    tiles = xres[:, g * GJ:(g + 1) * GJ, :]
                    ve.tensor_tensor(tiles, ps[:, BO:BO + 2, :].rearrange("p a (b x) -> p (a b) x", x=E), tiles, ALU.add)\
                        .then_inc(s["out_added"], 1)

                def slots(i, peeled):
                    for j in range(SLOTS):
                        hd, g = divmod(j, GROUPS)
                        first = peeled and j == 0
                        ve.wait_ge(s["v_made"], unit(att, i, j))
                        ve.tensor_tensor(v[:, j % 2], ps[:, BV, :].rearrange("p (t x) -> p t x", t=GJ),
                                         vb[:, hd:hd + 1, :].broadcast_to([P, GJ, K3]), ALU.add).then_inc(s["v_read"], 1)
                        if not first:
                            ctx_lo_part(i, j - 1)
                        ve.wait_ge(s["scores_made"], unit(att, i, j))
                        sp3 = ps[:, BS, 0:GJ * (L + 1)].rearrange("p (n x) -> p n x", n=GJ)
                        ve.tensor_reduce(r3[:, 0, :], sp3, AX, ALU.max)
                        ve.drain()
                        ve.tensor_tensor(e[:], sp3, r3[:, 0, :].unsqueeze(2).broadcast_to([P, GJ, L + 1]), ALU.subtract)\
                            .then_inc(s["less_made"], 1)
                        if not first:
                            add_out(i, j - 1)
                        ve.wait_ge(s["exp_made"], unit(att, i, j))
                        ve.tensor_reduce(r3[:, 1, :], e[:], AX, ALU.add)
                        ve.drain()
                        ve.reciprocal(r3[:, 2, :], r3[:, 1, :])
                        ve.drain()
                        ve.tensor_tensor(probs[:], e[:, :, 0:L], r3[:, 2, :].unsqueeze(2).broadcast_to([P, GJ, L]), ALU.mult)\
                            .then_inc(s["probs_made"], 1)

                turns(ve, att, slots)
                ctx_lo_part(ITER - 1, SLOTS - 1)
                add_out(ITER - 1, SLOTS - 1)
                ve.drain()

            for att in range(2):
                norm(att)
                attention(att)
            norm(2)
            for g in range(GROUPS):
                for f in range(FT):
                    m = g * FT + f
                    ve.wait_ge(s["gelu_made"], m + 1)
                    if m >= 2:
                        ve.wait_ge(s["fc2_made"], m - 1)
                    ve.tensor_copy(g_hi[:, m % 2, :], ge[:, m % 2, :])
                    ve.drain()
                    ve.tensor_tensor(g_lo[:, m % 2, :], ge[:, m % 2, :], g_hi[:, m % 2, :].bitcast(F32), ALU.subtract)\
                        .then_inc(s["gelu_split"], 1)
                ve.wait_ge(s["fc2_made"], (g + 1) * FT)
                tiles = xres[:, g * GJ:(g + 1) * GJ, :]
                ve.tensor_tensor(tiles, ps[:, 4:8, 0:E], tiles, ALU.add).then_inc(s["fc2_added"], 1)


def _halves(v):
    return v.reshape(C, P).T


def _kxm(w):
    return w.reshape(-1, P, w.shape[-1]).transpose(1, 0, 2)


def kernel(**a):
    import concourse.bacc as bacc
    from concourse.bass_utils import run_bass_kernel_spmd

    a = {n: np.asarray(v) for n, v in a.items()}
    l0, l1, l2, l3 = ({n[len(p):]: v for n, v in a.items() if n.startswith(p)}
                      for p in ("L0_xattn_", "L1_xattn_", "L2_xattn_", "L3_xattn_"))
    f32 = np.float32
    vectors = {n: l0[n] for n in ("ln1_w", "ln1_b", "ln2_w", "ln2_b", "maa_x", "time_decay", "gn_w", "gn_b",
                                  "ffn_maa_k", "ffn_maa_r")}
    vectors |= {f"stack{i}": l0["maa_stack"][i] for i in range(MIX)}
    vectors |= {"faaaa": l0["faaaa"].reshape(E), "ln_gamma": l1["ln_gamma"], "ln_beta": l1["ln_beta"]}
    vectors |= {"s1": l3["ln1_scale"], "o1": l3["ln1_offset"], "s2": l3["ln2_scale"], "o2": l3["ln2_offset"],
                "s3": l3["ln_mlp_scale"], "o3": l3["ln_mlp_offset"]}
    columns = [_halves(vectors[n]) for n in VECS]
    for at in ("1", "2"):
        columns += [l3[n + at].reshape(H3, K3).T for n in ("bq", "bk", "bias_k", "bias_v")]
    columns.append(l3["b_fc1"].reshape(FT, P).T)
    columns += [np.tile(l2[n], 2).reshape(P, 1) for n in ("bn", "bm", "bl", "bo")]
    even = (np.arange(P) // D1 % 2 == 0).astype(f32)
    columns += [even.reshape(P, 1), 1 - even.reshape(P, 1), np.broadcast_to(l1["gate"].reshape(1, 1), (P, 1))]
    cols = np.concatenate(columns, axis=1)

    square = [l0["Wr"].T, l0["Wk"].T, l0["Wv"].T, l0["Wg"].T, l0["Wo"].T, l0["ffn_Wk"].T, l0["ffn_Wr"].T,
              l0["ffn_Wv"].T, l1["Wq"].T, l1["Wk"].T, l1["Wv"].T, l1["Wo"].T]
    sq = np.stack([_kxm(w) for w in square], axis=1)
    n = np.arange(P)
    head = n[:, None] // S == n[None, :] // S
    spread = np.stack([head & (n[:, None] % S == d) for d in range(S)], axis=1).astype(f32)
    sel = np.stack([spread, spread.transpose(2, 1, 0)], axis=1)
    blocks = np.stack([head.astype(f32), head.astype(f32) / f32(S)], axis=1)
    w2l = np.zeros((P, 4, P), f32)
    for i, name in enumerate(("Wn", "Wm", "Wl", "Wo")):
        for o in (0, L):
            w2l[o:o + L, i, o:o + L] = l2[name].T
    wqkv = np.stack([np.stack([_kxm(l3[w + at]).reshape(P, C, H3, K3) for w in ("wq", "wk", "wv")], axis=1)
                     for at in ("1", "2")]).transpose(0, 4, 1, 2, 3, 5).reshape(2 * H3, P, 3 * C * K3)
    wo3 = np.concatenate([l3["wo" + at].reshape(H3, K3, E) for at in ("1", "2")])
    vrows = np.concatenate([np.stack([l3["bv" + at].reshape(H3, K3), l3["bias_v" + at].reshape(H3, K3)], axis=1)
                            for at in ("1", "2")])
    arrays = {
        "x": a["x"], "ctx": a["ctx_2048"], "mask": a["mask_BxS2_bf1"].view(np.uint8), "cols": cols, "sq": sq,
        "maa_w1": _kxm(l0["maa_w1"]), "maa_w2": l0["maa_w2"].reshape(MIX * LORA, E),
        "dec_w1": _kxm(l0["decay_w1"]), "dec_w2": l0["decay_w2"], "sel": sel, "blocks": blocks, "w2l": w2l,
        "rows3": np.stack([l3["bo1"], l3["bo2"], l3["b_fc2"]]), "wqkv": wqkv, "wo3": wo3, "vrows": vrows,
        "fc1": _kxm(l3["w_fc1"]), "fc2": _kxm(l3["w_fc2"]), "ident": np.eye(P, dtype=f32),
    }
    nc = bacc.Bacc("TRN2", target_bir_lowering=False, num_devices=1)
    ins, handles = {}, {}
    for name, v in arrays.items():
        ins[f"in_{name}"] = np.ascontiguousarray(v)
        handles[name] = nc.dram_tensor(f"in_{name}", v.shape, mybir.dt.from_np(v.dtype), kind="ExternalInput").ap()
    handles["out"] = nc.dram_tensor("out_0", (B, L, E), F32, kind="ExternalOutput").ap()
    program(nc, **handles)
    r = run_bass_kernel_spmd(nc, [ins], core_ids=[0])
    return r.results[0]["out_0"]
```

```python
from contextlib import ExitStack

import numpy as np

import concourse.bass as bass
from concourse import mybir

F32 = mybir.dt.float32
F32R = mybir.dt.float32r
U8 = mybir.dt.uint8
ACT = mybir.ActivationFunctionType
ALU = mybir.AluOpType
AX = mybir.AxisListType.X

P = 128
B, L, E = 32, 64, 256
C = E // P
NT = B * L // P
GB = 8
GT = GB * L
GJ = GT // P
GROUPS = B // GB
MB = 4
MT = MB * L
MJ = MT // P
TURNS = B // MB
S = 8
MIX = 5
MK, MW, MV, MR, MG = range(MIX)
LORA, DLORA = 32, 64
H1 = 16
D1 = E // H1
H3 = 16
K3 = 128
F3 = 1024
FT = F3 // P
WP = 2 * 3 * C * K3 + 2 * E
EPS = 1e-5
BANK = 512

VECS = ["ln1_w", "ln1_b", "ln2_w", "ln2_b", "maa_x", "stack0", "stack1", "stack2", "stack3", "stack4",
        "time_decay", "faaaa", "gn_w", "gn_b", "ffn_maa_k", "ffn_maa_r", "ln_gamma", "ln_beta",
        "s1", "o1", "s2", "o2", "s3", "o3"]
V0 = {n: 2 * i for i, n in enumerate(VECS)}
NV = 2 * len(VECS)
H0 = {(n, a): NV + (4 * a + m) * H3 for a in range(2) for m, n in enumerate(["bq", "bk", "bias_k", "bias_v"])}
FC0 = NV + 8 * H3
BN0 = FC0 + FT
BM0, BL0, BO0, EVEN0, GATE0 = BN0 + 1, BN0 + 2, BN0 + 3, BN0 + 4, BN0 + 6
NCOL = GATE0 + 1

STEPS_A = ["in", "x", "lora", "lora out", "project", "r", "g"] + [f"recur {d}" for d in range(S)] \
    + ["collect", "bonus", "mean", "var", "out", "ffn in", "shift", "ffn k", "ffn v"]
STEPS_B = ["in", "x2", "kv", "q", "scores 0", "scores 1", "softmax 0", "softmax 1", "turn 0", "turn 1", "heads 0",
           "heads 1", "out", "mix", "norm2", "mn", "scores2 0", "scores2 1", "softmax2 0", "turn2 0", "softmax2 1", "mix2 0", "turn2 1", "mix2 1", "end"]
TAKE = {
    "tensor": "bababababbabbaababaabababababbabbbaaaabbaabbababa",
    "scalar": "babababababbbaabababaabababababaababbaabbbabbaaab",
    "vector": "bababababbabababababaababaabbbabbaababababababbaa",
    "gpsimd": "abbbaababbabbaabbbaabaaabaabbbabbababbaaaabbbbaaa",
}
ORDER = {engine: [(p, (STEPS_A if p == "a" else STEPS_B)[take[:i].count(p)]) for i, p in enumerate(take)]
         for engine, take in TAKE.items()}

SQ = ["Wr", "Wk", "Wv", "Wg", "Wo", "fWk", "fWr", "fWv", "aWq", "aWk", "aWv", "aWo"]


class Steps:

    def __init__(self, semaphore, names):
        self.sem, self.names, self.next = semaphore, names, 0

    def one(self, name):
        assert self.names[self.next % len(self.names)] == name, (name, self.names[self.next % len(self.names)])
        self.next += 1
        return 1

    def at(self, turn, name):
        return turn * len(self.names) + self.names.index(name) + 1


def program(nc, x, ctx, mask, cols, sq, maa_w1, maa_w2, dec_w1, dec_w2, sel, blocks, w2l, rows3,
            w3, vrows, fc1, fc2, ident, out):
    xt = x.rearrange("b l e -> (b l) e").rearrange("(j p) e -> p j e", p=P)
    ct = ctx.rearrange("b l e -> (b l) e").rearrange("(j p) e -> p j e", p=P)
    ot = out.rearrange("b l e -> (b l) e").rearrange("(j p) e -> p j e", p=P)
    s0_dram = ctx[:, 2:2 + S, :].rearrange("b r e -> b (r e)").rearrange("b (c p d) -> p c b d", c=C, p=P)
    mask_pairs = mask.rearrange("(j o) l -> j o l", o=2)

    with ExitStack() as whole:
        def alloc(stack):
            return lambda name, shape, dt=F32: stack.enter_context(nc.sbuf_tensor(name, shape, dt))

        def sem(name):
            return whole.enter_context(nc.semaphore(name))

        keep = alloc(whole)
        ps = whole.enter_context(nc.psum_tensor("ps", [P, 8, BANK], F32))

        xres = keep("xres", [P, NT, E])
        ctx_hi = keep("ctx_hi", [P, C, B * L], F32R)
        ctx_lo = keep("ctx_lo", [P, C, B * L], F32R)
        col = keep("col", [P, NCOL])
        eye = keep("eye", [P, P])
        eps = keep("eps", [P, 1])
        brow = keep("brow", [P, 3, E])
        xres_mv = keep("xres_mv", [P, NT, 2])
        wraw = keep("wraw", [P, WP])
        vrow = keep("vrow", [P, 2, 2 * K3])

        def vec(name, c):
            return col[:, V0[name] + c:V0[name] + c + 1]

        mixers(nc, whole, alloc, sem, ps, locals())
        attention_mlp(nc, whole, alloc, sem, ps, locals())


def mixers(nc, whole, alloc, sem, ps, k):
    xres, xres_mv, ctx_hi, ctx_lo, col, eye, eps, vec = (
        k[n] for n in ("xres", "xres_mv", "ctx_hi", "ctx_lo", "col", "eye", "eps", "vec"))
    with ExitStack() as stack:
        sb = alloc(stack)
        wsq = sb("wsq", [P, len(SQ), C, E])
        w1m = sb("w1m", [P, C, MIX * LORA])
        w2m = sb("w2m", [P, 2, E])
        dw1 = sb("dw1", [P, C, DLORA])
        dw2 = sb("dw2", [DLORA, E])
        sel = sb("sel", [P, 2, S, P])
        blk = sb("blk", [P, 2, P])
        w2l = sb("w2l", [P, 4, P])
        s0 = sb("s0", [P, C, B, S])

        xin = sb("xin", [P, MJ, E])
        cin = sb("cin", [P, MJ, E])
        st = sb("st", [P, MJ, 6])
        mv = sb("mv", [P, MJ, 2])
        sd = sb("sd", [P, MJ])
        rs = sb("rs", [P, MJ])
        xn = sb("xn", [P, MJ, E])
        ctxT = sb("ctxT", [P, C, MT])
        xs = sb("xs", [P, C, MB, L + 1])
        sx = sb("sx", [P, C, MT])
        z = sb("z", [P, C, MT])
        th = sb("th", [P, 2, MT])
        mix = sb("mix", [P, MIX, C, MT])
        rT = sb("rT", [P, C, MT])
        kT = sb("kT", [P, C, MT])
        vT = sb("vT", [P, C, MT])
        v_hi = sb("v_hi", [P, C * MT], F32R)
        v_lo = sb("v_lo", [P, C * MT], F32R)
        spread = sb("spread", [P, S, P], F32R)
        gT = sb("gT", [P, C, MT])
        wsh = sb("wsh", [P, C, MB, L])
        dl = sb("dl", [DLORA, MT])
        kv = sb("kv", [P, 2, C, MB, L])
        sc = mix[:, 0:2]
        pr = mix[:, 2:4]
        x1 = sb("x1", [P, MJ, E])
        x2 = sb("x2", [P, MJ, E])
        cinb = sb("cinb", [P, MJ, E])
        masku = sb("masku", [P, MJ, L], U8)
        mbias = sb("mbias", [P, MJ, 2, L])
        stb = sb("stb", [P, MJ, 6])
        stx = sb("stx", [P, MJ, 6])
        mvx = sb("mvx", [P, MJ, 2])
        mvb = sb("mvb", [P, 2, MJ, 2])
        sdb = sb("sdb", [P, 2, MJ])
        rsb = sb("rsb", [P, 2, MJ])
        cn = sb("cn", [P, MJ, E])
        xnb = sb("xnb", [P, MJ, E])
        aT = sb("aT", [P, C, MT])
        x2T = sb("x2T", [P, C, MT])
        q1T = sb("q1T", [P, C, MT])
        ke = sb("ke", [P, C, MB, 2, L])
        v1 = sb("v1", [P, MB, E])
        probs = sb("probs", [P, 4, C * MT])
        probsT = sb("probsT", [P, 4, C * MT])
        oT = sb("oT", [P, C, MT])
        x3 = sb("x3", [P, MJ, E])
        mmT = sb("mmT", [P, MJ, E])
        mnT = sb("mnT", [P, MJ, E])
        mlT = sb("mlT", [P, MJ, E])
        moT = sb("moT", [P, MJ, E])
        tg = sb("tg", [P, 1])
        ROWS = 4 * C * MB
        red = sb("red", [P, 3, ROWS])
        red2 = sb("red2", [P, 4, 4 * MJ])
        p2 = probs[:].rearrange("p (j a) t -> p j (a t)", j=MJ)
        p2T = probsT[:].rearrange("p (j a) t -> p j (a t)", j=MJ)

        def seq(ap):
            return ap.rearrange("p (b l) -> p b l", b=MB)

        def seq2(ap):
            return ap.rearrange("p c (b l) -> p c b l", b=MB)

        def placed(ap):
            return ap.rearrange("p (r s l) -> p r s l", r=2, s=2)

        def by_batch(ap):
            return ap.rearrange("p (s r l) -> p r s l", r=2, s=2)

        def chan(bank):
            return ps[:, bank, :].rearrange("p (c t) -> p c t", c=C)

        def tok(bank):
            return ps[:, bank, :].rearrange("p (j e) -> p j e", e=E)

        cols_in, lora_in, wa_in, s0_in, wb_in = (sem(n + "_loaded") for n in ("columns", "lora", "weights_a", "states", "weights_b"))
        x_in, c_in, cb_in, m_in = sem("x_loaded"), sem("ctx_loaded"), sem("ctx_b_loaded"), sem("mask_loaded")
        ready, spread_ready = sem("constants_ready"), sem("spread_ready")
        w3_in = sem("layer3_weights_loaded")
        SQ_A = 8
        HALVES = range(C)
        D = range(S)
        SPREAD = [0, 1]
        MIX_G = 3
        PA = Steps(sem("tensor_a_steps"), ["ctx", "x", "lora in"] + [f"lora out {i}" for i in range(MIX)]
                   + ["decay in", "k", "v", "r", "decay out", "g"]
                   + [x for d in D for x in ([f"spread {d}"] + ([f"collect {d - 1}"] if d else []))] + [f"collect {S - 1}"]
                   + ["bonus", "mean", "var", "out", "x1", "ffn k", "ffn r", "ffn v"])
        AA = Steps(sem("scalar_a_steps"), ["sd", "ctxT", "xs", "th", "dl", "kT", "vT", "v hi", "rT", "decay e", "wsh", "gate tanh",
                                           "sq", "gn sd", "sd 1", "xs 1", "relu", "kk", "ffn tanh"])
        VA = Steps(sem("vector_a_steps"), ["xn", "prev", "z"] + [f"mixp {i}" for i in range(MIX)] + ["mix", "gate"]
                   + [x for d in D for x in (f"kv {d}", f"scan {d}")]
                   + ["ruk", "bonus v", "att", "cen", "y", "x1", "mv 1", "xn 1", "prev 1", "xr", "x2"])
        GA = Steps(sem("gpsimd_a_steps"), [f"mix {i}" for i in range(MIX_G)] + ["v lo", "first 0"]
                   + [x for d in D for x in ([f"first {d + 1}"] if d + 1 < S else []) + [f"read {d}"]] + ["ctx hi", "ctx lo"])
        VS = Steps(sem("vector_stat_steps"), ["mv a"])
        PB = Steps(sem("tensor_b_steps"), ["a", "x2", "k", "v", "q", "scores 0", "scores 1", "probs 0", "probs 1", "heads", "out", "mm", "ml", "mn"]
                   + [f"s2 {j}" for j in range(MJ)] + [x for j in range(MJ) for x in (f"p2 {j}", f"mo {j}")] + ["out 2"])
        AB = Steps(sem("scalar_b_steps"), ["sd", "aT", "x2T", "ke", "v1", "q", "exp 0", "exp 1", "probsT 0", "probsT 1", "oT", "mmT", "mlT", "sd 2",
                                           "mnT"] + [f"exp2 {j}" for j in range(MJ)] + [f"p2T {j}" for j in range(MJ)] + ["moT"])
        VB = Steps(sem("vector_b_steps"), ["mv", "cn", "less 0", "less 1", "probs 0", "probs 1", "x3", "mv 2", "xn 2"]
                   + [f"neg2 {j}" for j in range(MJ)] + [f"p2 {j}" for j in range(MJ)] + ["x4"])
        GB_ = Steps(sem("gpsimd_b_steps"), ["mask"])

        block = stack.enter_context(nc.Block())

        def weave(eng, name, part_a, part_b):
            def turn(g, with_a, with_b):
                a, b = part_a(g) if with_a else None, part_b(g - 1) if with_b else None
                a_next, b_next = next(a) if with_a else None, next(b) if with_b else None
                for part, step in ORDER[name]:
                    if part == "a" and step == a_next:
                        a_next = next(a, None)
                    if part == "b" and step == b_next:
                        b_next = next(b, None)
                assert a_next is None and b_next is None, (a_next, b_next)

            turn(0, True, False)
            with eng.Fori(1, TURNS) as g:
                turn(g, True, True)
            turn(TURNS, False, True)

        @block.sync
        def _(sp):
            def constants(signal, *copies):
                for dst, src in copies:
                    sp.dma_start(dst, src).then_inc(signal, 16)

            def load_a(g, first=False):
                if not first:
                    sp.wait_ge(VA.sem, VA.at(g - 1, "x1"))
                sp.dma_start(xin[:], k["xt"][:, bass.ds(g * MJ, MJ), :]).then_inc(x_in, 16)
                sp.dma_start(cin[:], k["ct"][:, bass.ds(g * MJ, MJ), :]).then_inc(c_in, 16)

            def load_b(g, first=False):
                if not first:
                    sp.wait_ge(PB.sem, PB.at(g - 1, "ml"))
                    sp.wait_ge(GB_.sem, GB_.at(g - 1, "mask"))
                sp.dma_start(cinb[:], k["ct"][:, bass.ds(g * MJ, MJ), :]).then_inc(cb_in, 16)
                for o in range(2):
                    sp.dma_start(masku[o * L:(o + 1) * L], k["mask_pairs"][bass.ds(g * MJ, MJ), o].partition_broadcast(L)).then_inc(m_in, 16)

            load_a(0, True)
            constants(cols_in, (eye[:], k["ident"]), (col[:], k["cols"]))
            constants(lora_in, (w1m[:], k["maa_w1"]), (w2m[:, 0], k["maa_w2"][0:P]), (w2m[0:LORA, 1], k["maa_w2"][P:P + LORA]),
                      (dw1[:], k["dec_w1"]), (dw2[:], k["dec_w2"]))
            constants(wa_in, (wsq[:, 0:SQ_A], k["sq"][:, 0:SQ_A]), (sel[:], k["sel"]), (blk[:], k["blocks"]))
            constants(s0_in, *((s0[:, c], k["s0_dram"][:, c]) for c in HALVES))
            load_b(0, True)
            constants(wb_in, (wsq[:, SQ_A:], k["sq"][:, SQ_A:]), (w2l[:], k["w2l"]))
            constants(w3_in, (k["brow"][:], k["rows3"].partition_broadcast(P)))
            with sp.Fori(1, TURNS) as g:
                load_a(g)
                load_b(g)
            sp.dma_start(k["wraw"][:], k["w3"][0]).then_inc(w3_in, 16)
            sp.dma_start(k["vrow"][:], k["vrows"][0].partition_broadcast(P)).then_inc(w3_in, 16)
            sp.wait_ge(w3_in, 48)

        @block.tensor
        def _(pe):
            def mm(out, lhsT, rhs, start=True, stop=True, **kw):
                return pe.matmul(out, lhsT, rhs, start=start, stop=stop, **kw)

            def turn_tiles(bank, src):
                for c in HALVES:
                    for j in range(MJ):
                        last = pe.transpose(chan(bank)[:, c, j * P:(j + 1) * P], src[:, j, c * P:(c + 1) * P], eye[:])
                return last

            def to_channels(bank, w, src):
                for m in HALVES:
                    for c in HALVES:
                        last = mm(chan(bank)[:, m, :], w[:, c, m * P:(m + 1) * P], src[:, c, :], c == 0, c == C - 1)
                return last

            def to_tokens(bank, w, src):
                for j in range(MJ):
                    for c in HALVES:
                        last = mm(tok(bank)[:, j, :], src[:, c, j * P:(j + 1) * P], w[:, c, :], c == 0, c == C - 1)
                return last

            W = {n: wsq[:, i] for i, n in enumerate(SQ)}

            def collect(g, d):
                pe.wait_ge(GA.sem, GA.at(g, f"read {d}"))
                for c in HALVES:
                    last = mm(chan(3)[:, c, :], sel[:, 1, d, :], pr[:, d % 2, c, :], d == 0 and c == 0, d == S - 1,
                              skip_group_check=True)
                last.then_inc(PA.sem, PA.one(f"collect {d}"))

            def keep_warm(n, bank=3):
                for _ in range(n):
                    mm(ps[:, bank, :], eye[:], wsq[:, 0:1].rearrange("p n c e -> p (n c e)"))

            def part_a(g):
                yield "in"
                pe.wait_ge(c_in, g * 16 + 16)
                turn_tiles(0, cin).then_inc(PA.sem, PA.one("ctx"))
                yield "x"
                pe.wait_ge(VA.sem, VA.at(g, "xn"))
                turn_tiles(1, xn).then_inc(PA.sem, PA.one("x"))
                yield "lora"
                pe.wait_ge(lora_in, 80)
                pe.wait_ge(VA.sem, VA.at(g, "z"))
                for c in HALVES:
                    mm(ps[:, 3, 0:MT], w1m[:, c, 0:P], z[:, c, :], c == 0, c == 1)
                for c in HALVES:
                    last = mm(ps[0:LORA, 3, MT:], w1m[:, c, P:P + LORA], z[:, c, :], c == 0, c == 1)
                last.then_inc(PA.sem, PA.one("lora in"))
                yield "lora out"
                pe.wait_ge(AA.sem, AA.at(g, "th"))
                for i in range(MIX):
                    if i >= 3:
                        pe.wait_ge(VA.sem, VA.at(g, f"mixp {i - 3}"))
                    at, part = (32 * i, 0) if i < 4 else (0, 1)
                    for c in HALVES:
                        last = mm(chan(i % 3)[:, c, :], w2m[at:at + LORA, part, c * P:(c + 1) * P], th[at:at + LORA, part, :])
                    last.then_inc(PA.sem, PA.one(f"lora out {i}"))
                yield "project"
                pe.wait_ge(wa_in, 48)
                pe.wait_ge(spread_ready, 1)
                pe.wait_ge(GA.sem, GA.at(g, f"mix {MIX_G - 1}"))
                for c in HALVES:
                    last = mm(ps[0:DLORA, 3, 0:MT], dw1[:, c, :], mix[:, MW, c, :], c == 0, c == 1)
                last.then_inc(PA.sem, PA.one("decay in"))
                to_channels(2, W["Wk"], mix[:, MK]).then_inc(PA.sem, PA.one("k"))
                pe.wait_ge(VA.sem, VA.at(g, "mixp 3"))
                to_channels(0, W["Wv"], mix[:, MV]).then_inc(PA.sem, PA.one("v"))
                yield "r"
                pe.wait_ge(AA.sem, AA.at(g, "dl"))
                pe.wait_ge(VA.sem, VA.at(g, "mix"))
                to_channels(3, W["Wr"], mix[:, MR]).then_inc(PA.sem, PA.one("r"))
                for m in HALVES:
                    last = mm(chan(1)[:, m, :], dw2[:, m * P:(m + 1) * P], dl[:])
                last.then_inc(PA.sem, PA.one("decay out"))
                yield "g"
                pe.wait_ge(AA.sem, AA.at(g, "kT"))
                to_channels(2, W["Wg"], mix[:, MG]).then_inc(PA.sem, PA.one("g"))

                for d in D:
                    yield f"recur {d}"
                    if d == 0:
                        pe.wait_ge(AA.sem, AA.at(g, "decay e"))
                        pe.wait_ge(GA.sem, GA.at(g, "v lo"))
                    if d >= 2:
                        pe.wait_ge(VA.sem, VA.at(g, f"kv {d - 2}"))
                    for n, part in enumerate((v_hi, v_lo)):
                        last = mm(ps[:, SPREAD[d % 2], :], spread[:, d, :], part[:], n == 0, n == 1)
                    last.then_inc(PA.sem, PA.one(f"spread {d}"))
                    if d >= 1:
                        collect(g, d - 1)
                yield "collect"
                collect(g, S - 1)
                yield "bonus"
                pe.wait_ge(VA.sem, VA.at(g, "ruk"))
                for c in HALVES:
                    last = mm(chan(2)[:, c, :], blk[:, 0, :], z[:, c, :])
                last.then_inc(PA.sem, PA.one("bonus"))
                yield "mean"
                keep_warm(1, 1)
                pe.wait_ge(VA.sem, VA.at(g, "att"))
                for c in HALVES:
                    last = mm(chan(0)[:, c, :], blk[:, 1, :], th[:, c, :])
                last.then_inc(PA.sem, PA.one("mean"))
                yield "var"
                pe.wait_ge(AA.sem, AA.at(g, "sq"))
                for c in HALVES:
                    last = mm(chan(1)[:, c, :], blk[:, 1, :], rT[:, c, :])
                last.then_inc(PA.sem, PA.one("var"))
                yield "out"
                pe.wait_ge(AA.sem, AA.at(g, "gn sd"))
                keep_warm(3)
                pe.wait_ge(VA.sem, VA.at(g, "y"))
                to_tokens(2, W["Wo"], z).then_inc(PA.sem, PA.one("out"))
                yield "ffn in"
                keep_warm(3)
                pe.wait_ge(VA.sem, VA.at(g, "xn 1"))
                turn_tiles(0, xn).then_inc(PA.sem, PA.one("x1"))
                yield "ffn k"
                pe.wait_ge(VA.sem, VA.at(g, "xr"))
                to_channels(1, W["fWk"], mix[:, 0]).then_inc(PA.sem, PA.one("ffn k"))
                to_tokens(3, W["fWr"], mix[:, 1]).then_inc(PA.sem, PA.one("ffn r"))
                yield "ffn v"
                pe.wait_ge(AA.sem, AA.at(g, "kk"))
                to_tokens(2, W["fWv"], kT).then_inc(PA.sem, PA.one("ffn v"))

            def part_b(g):
                yield "in"
                pe.wait_ge(VB.sem, VB.at(g, "cn"))
                turn_tiles(4, cn).then_inc(PB.sem, PB.one("a"))
                yield "x2"
                pe.wait_ge(VA.sem, VA.at(g, "x2"))
                turn_tiles(7, x2).then_inc(PB.sem, PB.one("x2"))
                yield "kv"
                pe.wait_ge(wb_in, 32)
                pe.wait_ge(AB.sem, AB.at(g, "aT"))
                to_channels(5, W["aWk"], aT).then_inc(PB.sem, PB.one("k"))
                for b in range(MB):
                    for e in range(2):
                        for c in HALVES:
                            last = mm(ps[e * L:(e + 1) * L, 6, b * P:(b + 1) * P], aT[:, c, b * L:(b + 1) * L],
                                      W["aWv"][:, c, :].rearrange("p (h e d) -> p h e d", e=2, d=D1)[:, :, e, :], c == 0, c == 1)
                last.then_inc(PB.sem, PB.one("v"))
                yield "q"
                pe.wait_ge(AB.sem, AB.at(g, "x2T"))
                to_channels(4, W["aWq"], x2T).then_inc(PB.sem, PB.one("q"))
                for i in range(2):
                    yield f"scores {i}"
                    if i == 0:
                        pe.wait_ge(AB.sem, AB.at(g, "q"))
                        pe.nop(nofuse=True)
                    for c in HALVES:
                        for b in range(MB):
                            for r in (2 * i, 2 * i + 1):
                                rows, o, at = slice(32 * r, 32 * r + 32), L * (b % 2), (c * MJ + b // 2) * P
                                last = mm(ps[o:o + L, 4 + r, at:at + P], q1T[rows, c, b * L:(b + 1) * L],
                                          ke[rows, c, b].rearrange("p e l -> p (e l)"))
                    last.then_inc(PB.sem, PB.one(f"scores {i}"))
                for i in range(2):
                    yield f"turn {i}"
                    pe.wait_ge(VB.sem, VB.at(g, f"probs {i}"))
                    for r in (2 * i, 2 * i + 1):
                        for n in range(C * MJ):
                            last = pe.transpose(ps[:, 4 + r, n * P:(n + 1) * P], probs[:, r, n * P:(n + 1) * P], eye[:])
                    last.then_inc(PB.sem, PB.one(f"probs {i}"))
                for c in HALVES:
                    yield f"heads {c}"
                    if c == 0:
                        pe.wait_ge(AB.sem, AB.at(g, "probsT 1"))
                        pe.nop(nofuse=True)
                    for b in range(MB):
                        for r in range(4):
                            at = (c * MJ + b // 2) * P + L * (b % 2)
                            last = mm(ps[32 * r:32 * r + 32, 4, c * MT + b * L:c * MT + (b + 1) * L],
                                      v1[:, b, c * P + 32 * r:c * P + 32 * r + 32], probsT[:, r, at:at + L])
                last.then_inc(PB.sem, PB.one("heads"))
                yield "out"
                pe.wait_ge(AB.sem, AB.at(g, "oT"))
                to_tokens(6, W["aWo"], oT).then_inc(PB.sem, PB.one("out"))
                yield "mix"
                for j in range(MJ):
                    last = mm(tok(4)[:, j, :], w2l[:, 1, :], cn[:, j, :])
                last.then_inc(PB.sem, PB.one("mm"))
                for j in range(MJ):
                    for h in range(2):
                        last = mm(tok(5)[:, j, h * P:(h + 1) * P], cinb[:, j, h * P:(h + 1) * P], w2l[:, 2, :])
                last.then_inc(PB.sem, PB.one("ml"))
                yield "mn"
                pe.wait_ge(VB.sem, VB.at(g, "xn 2"))
                for j in range(MJ):
                    last = mm(tok(6)[:, j, :], w2l[:, 0, :], xnb[:, j, :])
                last.then_inc(PB.sem, PB.one("mn"))
                for j in range(MJ):
                    yield f"scores2 {j}"
                    if j == 0:
                        pe.wait_ge(AB.sem, AB.at(g, "mnT"))
                    for o in range(2):
                        rows = slice(o * L, (o + 1) * L)
                        for h in range(2):
                            last = mm(ps[:, 4 + 2 * j + o, h * E:(h + 1) * E], mnT[rows, j, h * P:(h + 1) * P], mmT[rows, j, :])
                    last.then_inc(PB.sem, PB.one(f"s2 {j}"))
                for j in range(MJ):
                    yield f"turn2 {j}"
                    pe.wait_ge(VB.sem, VB.at(g, f"p2 {j}"))
                    for o in range(2):
                        for h in range(2):
                            for n in range(2):
                                at = o * 512 + h * E + n * P
                                last = pe.transpose(ps[:, 4 + 2 * j + o, n * E + h * P:n * E + (h + 1) * P],
                                                    p2[:, j, at:at + P], eye[:])
                    last.then_inc(PB.sem, PB.one(f"p2 {j}"))
                    yield f"mix2 {j}"
                    pe.wait_ge(AB.sem, AB.at(g, f"p2T {j}"))
                    for o in range(2):
                        for n in range(2):
                            last = mm(ps[o * L:(o + 1) * L, 4, j * E:(j + 1) * E], mlT[:, j, n * P + o * L:n * P + (o + 1) * L],
                                      p2T[:, j, o * 512 + n * E:o * 512 + (n + 1) * E], n == 0, n == 1)
                    last.then_inc(PB.sem, PB.one(f"mo {j}"))
                yield "end"
                pe.wait_ge(AB.sem, AB.at(g, "moT"))
                for j in range(MJ):
                    last = mm(tok(5)[:, j, :], w2l[:, 3, :], moT[:, j, :])
                last.then_inc(PB.sem, PB.one("out 2"))

            pe.wait_ge(cols_in, 32)
            pe.wait_ge(ready, 1)
            weave(pe, "tensor", part_a, part_b)

        @block.scalar
        def _(act):
            def affine_turned(bank, w, b):
                for c in HALVES:
                    last = act.activation(xs[:, c, :, 1:], seq(chan(bank)[:, c, :]), ACT.Identity, bias=vec(b, c), scale=vec(w, c))
                return last

            def part_a(g):
                yield "in"
                act.wait_ge(VS.sem, VS.at(g, "mv a"))
                act.activation(sd[:], mv[:, :, 1], ACT.Sqrt, bias=eps[:]).then_inc(AA.sem, AA.one("sd"))
                act.wait_ge(PA.sem, PA.at(g, "ctx"))
                act.copy(ctxT[:], chan(0)).then_inc(AA.sem, AA.one("ctxT"))
                yield "x"
                act.wait_ge(PA.sem, PA.at(g, "x"))
                affine_turned(1, "ln1_w", "ln1_b").then_inc(AA.sem, AA.one("xs"))
                yield "lora"
                act.wait_ge(PA.sem, PA.at(g, "lora in"))
                act.activation(th[:, 0, :], ps[:, 3, 0:MT], ACT.Tanh)
                act.activation(th[0:LORA, 1, :], ps[0:LORA, 3, MT:], ACT.Tanh).then_inc(AA.sem, AA.one("th"))
                yield "project"
                act.wait_ge(PA.sem, PA.at(g, "decay in"))
                act.activation(dl[:], ps[0:DLORA, 3, 0:MT], ACT.Tanh).then_inc(AA.sem, AA.one("dl"))
                act.wait_ge(PA.sem, PA.at(g, "k"))
                act.copy(kT[:], chan(2)).then_inc(AA.sem, AA.one("kT"))
                act.wait_ge(PA.sem, PA.at(g, "v"))
                act.copy(vT[:], chan(0)).then_inc(AA.sem, AA.one("vT"))
                act.copy(v_hi[:], ps[:, 0, :]).then_inc(AA.sem, AA.one("v hi"))
                yield "r"
                act.wait_ge(PA.sem, PA.at(g, "r"))
                act.copy(rT[:], chan(3)).then_inc(AA.sem, AA.one("rT"))
                act.wait_ge(PA.sem, PA.at(g, "decay out"))
                for c in HALVES:
                    last = act.activation(sx[:, c, :], chan(1)[:, c, :], ACT.Exp, bias=vec("time_decay", c))
                last.then_inc(AA.sem, AA.one("decay e"))
                act.drain()
                act.activation(wsh[:, :, :, 1:], seq2(sx[:])[:, :, :, 0:L - 1], ACT.Exp, scale=-1.0).then_inc(AA.sem, AA.one("wsh"))
                yield "g"
                act.wait_ge(PA.sem, PA.at(g, "g"))
                act.activation(gT[:], chan(2), ACT.Tanh, scale=0.5).then_inc(AA.sem, AA.one("gate tanh"))
                yield "mean"
                act.wait_ge(VA.sem, VA.at(g, "cen"))
                act.activation(rT[:], kT[:], ACT.Square).then_inc(AA.sem, AA.one("sq"))
                yield "var"
                act.wait_ge(PA.sem, PA.at(g, "var"))
                act.activation(vT[:], chan(1), ACT.Sqrt, bias=eps[:]).then_inc(AA.sem, AA.one("gn sd"))
                yield "ffn in"
                act.wait_ge(GA.sem, GA.at(g, "ctx lo"))
                act.wait_ge(VA.sem, VA.at(g, "mv 1"))
                act.activation(sd[:], mv[:, :, 1], ACT.Sqrt, bias=eps[:]).then_inc(AA.sem, AA.one("sd 1"))
                act.wait_ge(PA.sem, PA.at(g, "x1"))
                affine_turned(0, "ln2_w", "ln2_b").then_inc(AA.sem, AA.one("xs 1"))
                yield "ffn k"
                act.wait_ge(PA.sem, PA.at(g, "ffn k"))
                act.activation(rT[:], chan(1), ACT.Relu).then_inc(AA.sem, AA.one("relu"))
                act.drain()
                act.activation(kT[:], rT[:], ACT.Square).then_inc(AA.sem, AA.one("kk"))
                act.wait_ge(PA.sem, PA.at(g, "ffn r"))
                act.activation(gT[:], chan(3), ACT.Tanh, scale=0.5).then_inc(AA.sem, AA.one("ffn tanh"))

            def part_b(g):
                yield "in"
                act.wait_ge(VB.sem, VB.at(g, "mv"))
                act.activation(sdb[:, 0, :], mvb[:, 0, :, 1], ACT.Sqrt, bias=eps[:]).then_inc(AB.sem, AB.one("sd"))
                act.wait_ge(PB.sem, PB.at(g, "a"))
                for c in HALVES:
                    last = act.activation(aT[:, c, :], chan(4)[:, c, :], ACT.Identity, bias=vec("ln_beta", c), scale=vec("ln_gamma", c))
                last.then_inc(AB.sem, AB.one("aT"))
                yield "x2"
                act.wait_ge(PB.sem, PB.at(g, "x2"))
                act.copy(x2T[:], chan(7)).then_inc(AB.sem, AB.one("x2T"))
                yield "kv"
                act.wait_ge(PB.sem, PB.at(g, "k"))
                for e in range(2):
                    last = act.activation(ke[:].rearrange("p c b e l -> p (c b) e l")[:, :, e, :],
                                          ps[:, 5, :].rearrange("p (n l) -> p n l", l=L), ACT.Copy,
                                          scale=col[:, EVEN0 + e:EVEN0 + e + 1])
                last.then_inc(AB.sem, AB.one("ke"))
                act.wait_ge(PB.sem, PB.at(g, "v"))
                for e in range(2):
                    half = slice(e * L, (e + 1) * L)
                    last = act.copy(v1[half].rearrange("p b (h e d) -> p (b h) e d", e=2, d=D1)[:, :, e, :],
                                    ps[half, 6, :].rearrange("p (n d) -> p n d", d=D1))
                last.then_inc(AB.sem, AB.one("v1"))
                yield "q"
                act.wait_ge(PB.sem, PB.at(g, "q"))
                act.copy(q1T[:], chan(4)).then_inc(AB.sem, AB.one("q"))
                for i in range(2):
                    yield f"scores {i}"
                    act.wait_ge(VB.sem, VB.at(g, f"less {i}"))
                    rows = probs[:, 2 * i:2 * i + 2]
                    act.activation(rows, rows, ACT.Exp).then_inc(AB.sem, AB.one(f"exp {i}"))
                for i in range(2):
                    yield f"turn {i}"
                    act.wait_ge(PB.sem, PB.at(g, f"probs {i}"))
                    act.copy(probsT[:, 2 * i:2 * i + 2], ps[:, 4 + 2 * i:6 + 2 * i, :]).then_inc(AB.sem, AB.one(f"probsT {i}"))
                yield "heads 1"
                act.wait_ge(PB.sem, PB.at(g, "heads"))
                act.copy(oT[:], chan(4)).then_inc(AB.sem, AB.one("oT"))
                yield "mix"
                act.wait_ge(PB.sem, PB.at(g, "mm"))
                act.activation(mmT[:], tok(4), ACT.Identity, bias=col[:, BM0:BM0 + 1]).then_inc(AB.sem, AB.one("mmT"))
                act.wait_ge(PB.sem, PB.at(g, "ml"))
                act.copy(mlT[:], tok(5)).then_inc(AB.sem, AB.one("mlT"))
                yield "norm2"
                act.wait_ge(VB.sem, VB.at(g, "mv 2"))
                act.activation(sdb[:, 1, :], mvb[:, 1, :, 1], ACT.Sqrt, bias=eps[:]).then_inc(AB.sem, AB.one("sd 2"))
                yield "mn"
                act.wait_ge(PB.sem, PB.at(g, "mn"))
                act.activation(mnT[:], tok(6), ACT.Identity, bias=col[:, BN0:BN0 + 1]).then_inc(AB.sem, AB.one("mnT"))
                for j in range(MJ):
                    yield f"scores2 {j}"
                    act.wait_ge(VB.sem, VB.at(g, f"neg2 {j}"))
                    for n in range(4):
                        last = act.activation(p2[:, j, n * E:(n + 1) * E], ps[:, 4 + 2 * j + n // 2, (n % 2) * E:(n % 2 + 1) * E],
                                              ACT.Exp, bias=red2[:, 0, 4 * j + n:4 * j + n + 1],
                                              accum_out=red2[:, 1, 4 * j + n:4 * j + n + 1])
                    last.then_inc(AB.sem, AB.one(f"exp2 {j}"))
                for j in range(MJ):
                    yield f"turn2 {j}"
                    act.wait_ge(PB.sem, PB.at(g, f"p2 {j}"))
                    act.copy(p2T[:, j, :], ps[:, 4 + 2 * j:6 + 2 * j, :].rearrange("p o t -> p (o t)"))\
                        .then_inc(AB.sem, AB.one(f"p2T {j}"))
                yield "mix2 1"
                act.wait_ge(PB.sem, PB.at(g, f"mo {MJ - 1}"))
                act.activation(moT[:], tok(4), ACT.Identity, bias=col[:, BL0:BL0 + 1]).then_inc(AB.sem, AB.one("moT"))

            act.wait_ge(cols_in, 32)
            act.wait_ge(ready, 1)
            act.activation(tg[:], col[:, GATE0:GATE0 + 1], ACT.Tanh).then_inc(ready, 1)
            weave(act, "scalar", part_a, part_b)

        @block.vector
        def _(ve):
            p3 = probs[:].rearrange("p r (n l) -> p (r n) l", l=L)
            mask_row = mbias[:].rearrange("p j e l -> p (j e l)").unsqueeze(1)

            def over(numbers):
                return numbers.unsqueeze(2).broadcast_to([P, ROWS // 2, L])

            def stats(stat, mean_var, src):
                for j in range(MJ):
                    ve.bn_stats(stat[:, j, :], src[:, j, :])
                ve.drain()
                for j in range(MJ):
                    last = ve.bn_aggr(mean_var[:, j, :], stat[:, j, :])
                return last

            def normalise(dst, src, mean_var, dev, inv):
                ve.reciprocal(inv, dev)
                ve.drain()
                for j in range(MJ):
                    last = ve.tensor_scalar(dst[:, j, :], src[:, j, :], mean_var[:, j, 0:1], inv[:, j:j + 1],
                                            ALU.subtract, ALU.mult)
                return last

            def shift(g, row, prev, producer):
                ve.tensor_copy(xs[:, :, :, 0:1], seq2(ctxT[:])[:, :, :, row:row + 1]).then_inc(VA.sem, VA.one(prev))
                ve.drain()
                ve.wait_ge(AA.sem, AA.at(g, producer))
                ve.tensor_tensor(seq2(sx[:]), xs[:, :, :, 0:L], xs[:, :, :, 1:], ALU.subtract)
                ve.drain()

            def mixed(dst, name):
                for c in HALVES:
                    last = ve.scalar_tensor_tensor(seq(dst[:, c, :]), seq(sx[:, c, :]), vec(name, c), xs[:, c, :, 1:],
                                                   ALU.mult, ALU.add)
                return last

            def part_a(g):
                yield "in"
                ve.wait_ge(x_in, g * 16 + 16)
                stats(st, mv, xin).then_inc(VS.sem, VS.one("mv a"))
                ve.wait_ge(AA.sem, AA.at(g, "sd"))
                normalise(xn, xin, mv, sd[:], rs[:]).then_inc(VA.sem, VA.one("xn"))
                yield "x"
                ve.wait_ge(AA.sem, AA.at(g, "ctxT"))
                shift(g, 1, "prev", "xs")
                mixed(z, "maa_x").then_inc(VA.sem, VA.one("z"))
                yield "lora out"
                for i in range(MIX):
                    ve.wait_ge(PA.sem, PA.at(g, f"lora out {i}"))
                    for c in HALVES:
                        last = ve.scalar_tensor_tensor(mix[:, i, c, :], chan(i % 3)[:, c, :], vec(f"stack{i}", c), sx[:, c, :],
                                                       ALU.add, ALU.mult)
                    last.then_inc(VA.sem, VA.one(f"mixp {i}"))
                ve.drain()
                for i in range(MIX_G, MIX):
                    last = ve.tensor_tensor(seq2(mix[:, i]), seq2(mix[:, i]), xs[:, :, :, 1:], ALU.add)
                last.then_inc(VA.sem, VA.one("mix"))
                yield "g"
                ve.wait_ge(AA.sem, AA.at(g, "gate tanh"))
                ve.scalar_tensor_tensor(gT[:], gT[:], 1.0, chan(2), ALU.add, ALU.mult).then_inc(VA.sem, VA.one("gate"))

                for d in D:
                    yield f"recur {d}"
                    ve.wait_ge(PA.sem, PA.at(g, f"spread {d}"))
                    for c in HALVES:
                        last = ve.tensor_tensor(kv[:, d % 2, c, :, 1:], seq(kT[:, c, :])[:, :, 0:L - 1],
                                                seq(chan(SPREAD[d % 2])[:, c, :])[:, :, 0:L - 1], ALU.mult)
                    last.then_inc(VA.sem, VA.one(f"kv {d}"))
                    ve.drain()
                    ve.wait_ge(GA.sem, GA.at(g, f"first {d}"))
                    if d >= 2:
                        ve.wait_ge(GA.sem, GA.at(g, f"read {d - 2}"))
                    ve.tensor_tensor_scan(sc[:, d % 2].rearrange("p c t -> p (c t)"), wsh[:].rearrange("p c b l -> p (c b l)"),
                                          kv[:, d % 2].rearrange("p c b l -> p (c b l)"), 0.0, ALU.mult, ALU.add)\
                        .then_inc(VA.sem, VA.one(f"scan {d}"))
                yield "bonus"
                for c in HALVES:
                    last = ve.scalar_tensor_tensor(z[:, c, :], rT[:, c, :], vec("faaaa", c), kT[:, c, :], ALU.mult, ALU.mult)
                last.then_inc(VA.sem, VA.one("ruk"))
                ve.wait_ge(PA.sem, PA.at(g, "bonus"))
                ve.tensor_tensor(sx[:], chan(2), vT[:], ALU.mult).then_inc(VA.sem, VA.one("bonus v"))
                yield "mean"
                ve.drain()
                ve.wait_ge(PA.sem, PA.at(g, f"collect {S - 1}"))
                ve.tensor_tensor(th[:], chan(3), sx[:], ALU.add).then_inc(VA.sem, VA.one("att"))
                ve.drain()
                ve.wait_ge(PA.sem, PA.at(g, "mean"))
                ve.tensor_tensor(kT[:], th[:], chan(0), ALU.subtract).then_inc(VA.sem, VA.one("cen"))
                ve.drain()
                for c in HALVES:
                    ve.scalar_tensor_tensor(z[:, c, :], kT[:, c, :], vec("gn_w", c), gT[:, c, :], ALU.mult, ALU.mult)
                    ve.tensor_scalar(gT[:, c, :], gT[:, c, :], vec("gn_b", c), None, ALU.mult)
                yield "var"
                ve.wait_ge(AA.sem, AA.at(g, "gn sd"))
                ve.reciprocal(vT[:], vT[:])
                ve.drain()
                ve.tensor_tensor(z[:], z[:], vT[:], ALU.mult)
                ve.drain()
                ve.tensor_tensor(z[:], z[:], gT[:], ALU.add).then_inc(VA.sem, VA.one("y"))
                yield "out"
                ve.wait_ge(PA.sem, PA.at(g, "out"))
                ve.scalar_tensor_tensor(x1[:], tok(2), 0.5, xin[:], ALU.mult, ALU.add).then_inc(VA.sem, VA.one("x1"))
                yield "ffn in"
                ve.drain()
                stats(st, mv, x1).then_inc(VA.sem, VA.one("mv 1"))
                ve.wait_ge(AA.sem, AA.at(g, "sd 1"))
                normalise(xn, x1, mv, sd[:], rs[:]).then_inc(VA.sem, VA.one("xn 1"))
                yield "shift"
                shift(g, 0, "prev 1", "xs 1")
                mixed(mix[:, 0], "ffn_maa_k")
                mixed(mix[:, 1], "ffn_maa_r").then_inc(VA.sem, VA.one("xr"))
                yield "ffn v"
                ve.wait_ge(PA.sem, PA.at(g, "ffn v"))
                ve.wait_ge(AA.sem, AA.at(g, "ffn tanh"))
                halves = vT[:].rearrange("p c t -> p (c t)").rearrange("p (j e) -> p j e", e=E)
                ve.scalar_tensor_tensor(halves, gT[:].rearrange("p c t -> p (c t)").rearrange("p (j e) -> p j e", e=E), 1.0,
                                        tok(2), ALU.add, ALU.mult)
                ve.drain()
                ve.scalar_tensor_tensor(x2[:], halves, 0.5, x1[:], ALU.mult, ALU.add).then_inc(VA.sem, VA.one("x2"))

            def part_b(g):
                yield "in"
                ve.wait_ge(cb_in, g * 16 + 16)
                stats(stb, mvb[:, 0], cinb).then_inc(VB.sem, VB.one("mv"))
                ve.wait_ge(AB.sem, AB.at(g, "sd"))
                normalise(cn, cinb, mvb[:, 0], sdb[:, 0, :], rsb[:, 0]).then_inc(VB.sem, VB.one("cn"))
                rows = [slice(i * ROWS // 2, (i + 1) * ROWS // 2) for i in range(2)]
                for i in range(2):
                    yield f"scores {i}"
                    ve.wait_ge(PB.sem, PB.at(g, f"scores {i}"))
                    if i == 0:
                        ve.wait_ge(GB_.sem, GB_.at(g, "mask"))
                    two = slice(2 * i, 2 * i + 2)
                    for c in HALVES:
                        ve.scalar_tensor_tensor(probs[:, two, c * MT:(c + 1) * MT], ps[:, 4 + 2 * i:6 + 2 * i, c * MT:(c + 1) * MT],
                                                float(D1) ** -0.5, mask_row.broadcast_to([P, 2, MT]), ALU.mult, ALU.add)
                    ve.drain()
                    ve.tensor_reduce(red[:, 0, rows[i]], p3[:, rows[i]], AX, ALU.max)
                    ve.drain()
                    ve.tensor_tensor(p3[:, rows[i]], p3[:, rows[i]], over(red[:, 0, rows[i]]), ALU.subtract)\
                        .then_inc(VB.sem, VB.one(f"less {i}"))
                for i in range(2):
                    yield f"softmax {i}"
                    ve.wait_ge(AB.sem, AB.at(g, f"exp {i}"))
                    ve.tensor_reduce(red[:, 1, rows[i]], p3[:, rows[i]], AX, ALU.add)
                    ve.drain()
                    ve.reciprocal(red[:, 2, rows[i]], red[:, 1, rows[i]])
                    ve.drain()
                    ve.tensor_tensor(p3[:, rows[i]], p3[:, rows[i]], over(red[:, 2, rows[i]]), ALU.mult)\
                        .then_inc(VB.sem, VB.one(f"probs {i}"))
                yield "out"
                ve.wait_ge(PB.sem, PB.at(g, "out"))
                ve.scalar_tensor_tensor(x3[:], tok(6), tg[:], x2[:], ALU.mult, ALU.add).then_inc(VB.sem, VB.one("x3"))
                ve.drain()
                stats(stb, mvb[:, 1], x3).then_inc(VB.sem, VB.one("mv 2"))
                yield "norm2"
                ve.wait_ge(AB.sem, AB.at(g, "sd 2"))
                normalise(xnb, x3, mvb[:, 1], sdb[:, 1, :], rsb[:, 1]).then_inc(VB.sem, VB.one("xn 2"))
                for j in range(MJ):
                    yield f"scores2 {j}"
                    at = slice(4 * j, 4 * j + 4)
                    ve.wait_ge(PB.sem, PB.at(g, f"s2 {j}"))
                    ve.tensor_reduce(red2[:, 2, at], ps[:, 4 + 2 * j:6 + 2 * j, :].rearrange("p o (h e) -> p (o h) e", e=E), AX, ALU.max)
                    ve.drain()
                    ve.tensor_scalar(red2[:, 0, at], red2[:, 2, at], -1.0, None, ALU.mult).then_inc(VB.sem, VB.one(f"neg2 {j}"))
                for j in range(MJ):
                    yield f"softmax2 {j}"
                    at = slice(4 * j, 4 * j + 4)
                    ve.wait_ge(AB.sem, AB.at(g, f"exp2 {j}"))
                    ve.reciprocal(red2[:, 3, at], red2[:, 1, at])
                    ve.drain()
                    rows = p2[:, j, :].rearrange("p (n e) -> p n e", e=E)
                    ve.tensor_tensor(rows, rows, red2[:, 3, at].unsqueeze(2).broadcast_to([P, 4, E]), ALU.mult)\
                        .then_inc(VB.sem, VB.one(f"p2 {j}"))
                yield "end"
                ve.wait_ge(PB.sem, PB.at(g, "out 2"))
                ve.scalar_tensor_tensor(xres[:, bass.ds(g * MJ, MJ), :], tok(5), col[:, BO0:BO0 + 1], x3[:], ALU.add, ALU.add)\
                    .then_inc(VB.sem, VB.one("x4"))
                ve.drain()
                for j in range(MJ):
                    ve.bn_stats(stx[:, j, :], xres[:, bass.ds(g * MJ + j, 1), :])
                ve.drain()
                for j in range(MJ):
                    ve.bn_aggr(mvx[:, j, :], stx[:, j, :])
                ve.drain()
                ve.tensor_copy(xres_mv[:, bass.ds(g * MJ, MJ), :], mvx[:])

            ve.memset(eps[:], EPS)
            ve.memset(wsh[:], 0.0)
            ve.memset(v1[:], 0.0).then_inc(ready, 1)
            ve.wait_ge(cols_in, 32)
            ve.wait_ge(ready, 2)
            weave(ve, "vector", part_a, part_b)
            ve.drain()

        @block.gpsimd
        def _(gp):
            def first(g, d):
                if d >= 2:
                    gp.wait_ge(VA.sem, VA.at(g, f"scan {d - 2}"))
                    gp.nop(nofuse=True)
                gp.tensor_copy(kv[:, d % 2, :, :, 0:1], s0[:, :, bass.ds(g * MB, MB), d:d + 1]).then_inc(GA.sem, GA.one(f"first {d}"))

            def part_a(g):
                yield "lora out"
                for i in range(MIX_G):
                    gp.wait_ge(VA.sem, VA.at(g, f"mixp {i}"))
                    gp.tensor_tensor(seq2(mix[:, i]), seq2(mix[:, i]), xs[:, :, :, 1:], ALU.add).then_inc(GA.sem, GA.one(f"mix {i}"))

                yield "r"
                gp.wait_ge(AA.sem, AA.at(g, "v hi"))
                gp.tensor_tensor(v_lo[:], vT[:].rearrange("p c t -> p (c t)"), v_hi[:].bitcast(F32), ALU.subtract)\
                    .then_inc(GA.sem, GA.one("v lo"))
                for d in D:
                    yield f"recur {d}"
                    if d == 0:
                        gp.wait_ge(AA.sem, AA.at(g, "rT"))
                        gp.nop(nofuse=True)
                        first(g, 0)
                    if d + 1 < S:
                        first(g, d + 1)
                    gp.wait_ge(VA.sem, VA.at(g, f"scan {d}"))
                    if d >= 2:
                        gp.wait_ge(PA.sem, PA.at(g, f"collect {d - 2}"))
                    gp.tensor_tensor(pr[:, d % 2], rT[:], sc[:, d % 2], ALU.mult).then_inc(GA.sem, GA.one(f"read {d}"))
                yield "bonus"
                gp.wait_ge(AA.sem, AA.at(g, "ctxT"))
                gp.nop(nofuse=True)
                where = bass.ds(g * MT, MT)
                pieces = [(placed(ctx_hi[:, c, where]), placed(ctx_lo[:, c, where]), by_batch(ctxT[:, c, :])) for c in HALVES]
                for hi, lo, source in pieces:
                    last = gp.tensor_copy(hi, source)
                last.then_inc(GA.sem, GA.one("ctx hi"))
                gp.drain()
                for hi, lo, source in pieces:
                    last = gp.tensor_tensor(lo, source, hi.bitcast(F32), ALU.subtract)
                last.then_inc(GA.sem, GA.one("ctx lo"))

            def part_b(g):
                yield "in"
                gp.wait_ge(m_in, g * 32 + 32)
                gp.nop(nofuse=True)
                gp.tensor_scalar(mbias[:], masku[:].unsqueeze(2).broadcast_to([P, MJ, 2, L]), 1.0, 3e38, ALU.subtract, ALU.mult)
                gp.drain()
                gp.tensor_scalar(mbias[:], mbias[:], 10.0, None, ALU.mult).then_inc(GB_.sem, GB_.one("mask"))

            gp.wait_ge(wa_in, 48)
            gp.tensor_copy(spread[:], sel[:, 0]).then_inc(spread_ready, 1)
            gp.wait_ge(s0_in, 32)
            weave(gp, "gpsimd", part_a, part_b)


def attention_mlp(nc, whole, alloc, sem, ps, k):
    xres, ctx_hi, ctx_lo, col, eye, eps, brow, vec, mv, wraw, vrow = (k[n] for n in (
        "xres", "ctx_hi", "ctx_lo", "col", "eye", "eps", "brow", "vec", "xres_mv", "wraw", "vrow"))
    with ExitStack() as stack:
        sb = alloc(stack)
        h_hi = sb("h_hi", [P, C, B * L], F32R)
        h_lo = sb("h_lo", [P, C, B * L], F32R)
        xn = sb("xn3", [P, NT, E])
        v = sb("v3", [P, 2, GJ, 2 * K3])
        st = sb("st3", [P, NT, 6])
        sd = sb("sd3", [P, NT])
        rs = sb("rs3", [P, NT])
        WQ, WK, WV, WO = 0, 2 * C * K3, 4 * C * K3, 6 * C * K3
        w_hi = sb("w_hi", [P, 2, WP], F32R)
        w_lo = sb("w_lo", [P, 2, WP], F32R)
        vb = sb("vb", [P, 2, 2 * K3])
        qT = sb("qT", [P, GT])
        kT = sb("k3T", [P, 2, GB, L + 1])
        e = sb("e3", [P, GJ, L + 1])
        probs = sb("probs3", [P, GJ, L])
        r3 = sb("r3", [P, 3, GJ])
        pT = sb("pT", [P, GJ, P])
        c_hi = sb("c_hi", [P, GT], F32R)
        c_lo = sb("c_lo", [P, GT], F32R)
        f1raw = xn[:, 0:NT // 2, :].rearrange("p j e -> p (j e)").rearrange("p (c f) -> p c f", c=C)
        f2raw = xn[:, NT // 2:, :]
        f1_hi = sb("f1_hi", [P, C, F3], F32R)
        f1_lo = sb("f1_lo", [P, C, F3], F32R)
        f2_hi = sb("f2_hi", [P, FT, E], F32R)
        f2_lo = sb("f2_lo", [P, FT, E], F32R)
        hb = sb("hb", [P, 2, 4, 2])
        ge = sb("ge", [P, 2, GT])
        g_hi = ctx_hi[:, 0, 0:2 * GT].rearrange("p (n t) -> p n t", n=2)
        g_lo = ctx_lo[:, 0, 0:2 * GT].rearrange("p (n t) -> p n t", n=2)

        PAIRS = H3 // 2
        PSLOTS = 2 * GROUPS
        ITER = PAIRS // 2
        SLOTS = 2 * PSLOTS
        UNITS = ITER * SLOTS
        BQ, BK, BV, BS, BC, BO = 0, 1, 2, 3, 5, 6
        SW = E
        s = {n: sem(n) for n in """stats_made first_hi_made w_loaded w_ready f_loaded f_ready blocks_clear
            q_made q_read k_made k_read v_made v_read scores_made less_made exp_made probs_made
            probs_turned pT_read ctx_made ctx_hi_made ctx_lo_made out_made out_added
            fc1_made gelu_made gelu_split fc2_made fc2_added stored""".split()}
        LP = Steps(sem("norm_tensor_steps"), [f"turned {g}" for g in range(GROUPS)])
        LA = Steps(sem("norm_scalar_steps"), [f"sd {g}" for g in range(GROUPS)] + [f"hT {g}" for g in range(GROUPS)])
        LV = Steps(sem("norm_vector_steps"), ["xn 0", "xn 1", "xn 2", "split 0", "xn 3", "split 1", "split 2", "split 3"])

        def tiles(g):
            return slice(g * GJ, (g + 1) * GJ)

        def turned(g):
            return xn[:, tiles(g), :].rearrange("p j e -> p (j e)").rearrange("p (c t) -> p c t", c=C)

        def parts(j):
            return j % SLOTS // PSLOTS, j % PSLOTS // 2, j % 2

        def unit(att, i, j):
            return i * SLOTS + (att * UNITS + j + 1)

        def added(att, i, j):
            return i * (SLOTS // 2) + (att * (UNITS // 2) + (j + 1) // 2)

        def turns(eng, slots):
            slots(0, True, False)
            with eng.Fori(1, ITER - 1) as i:
                slots(i, False, False)
            slots(ITER - 1, False, True)

        def passes(a_hi, a_lo, b_hi, b_lo):
            return ((a_hi, b_hi), (a_hi, b_lo), (a_lo, b_hi))

        block = stack.enter_context(nc.Block())

        @block.sync
        def _(sp):
            def pair(at):
                sp.wait_ge(s["w_ready"], at)
                sp.dma_start(wraw[:], k["w3"][bass.ds(at, 1)]).then_inc(s["w_loaded"], 16)
                sp.dma_start(vrow[:], k["vrows"][bass.ds(at, 1)].partition_broadcast(P)).then_inc(s["w_loaded"], 16)

            with sp.Fori(1, 2 * PAIRS - 1) as n:
                pair(n)
            sp.wait_ge(LV.sem, LV.at(1, f"split {GROUPS - 1}"))
            sp.dma_start(f1raw, k["fc1"]).then_inc(s["f_loaded"], 16)
            sp.dma_start(f2raw, k["fc2"]).then_inc(s["f_loaded"], 16)
            pair(2 * PAIRS - 1)
            for g in range(GROUPS):
                sp.wait_ge(s["fc2_added"], g + 1)
                sp.dma_start(k["ot"][:, g * GJ:(g + 1) * GJ, :], xres[:, g * GJ:(g + 1) * GJ, :]).then_inc(s["stored"], 16)
            sp.wait_ge(s["stored"], 16 * GROUPS)

        @block.gpsimd
        def _(gp):
            def pair(par, n, first=False):
                if first and n == 0:
                    gp.wait_ge(s["first_hi_made"], 1)
                else:
                    gp.wait_ge(s["w_loaded"], n * 32)
                    if not first:
                        gp.wait_ge(s["out_made"], n * PSLOTS - PSLOTS)
                    gp.nop(nofuse=True)
                    gp.tensor_copy(w_hi[:, par, :], wraw[:])
                gp.tensor_tensor(vb[:, par, :], vrow[:, 0, :], vrow[:, 1, :], ALU.subtract)
                gp.drain()
                gp.tensor_tensor(w_lo[:, par, :], wraw[:], w_hi[:, par, :].bitcast(F32), ALU.subtract)\
                    .then_inc(s["w_ready"], 1)

            gp.memset(pT[:], 0.0).then_inc(s["blocks_clear"], 1)
            pair(0, 0, True)
            pair(1, 1, True)
            with gp.Fori(1, PAIRS) as i:
                for par in range(2):
                    pair(par, i * 2 + par, False)
            gp.wait_ge(s["f_loaded"], 32)
            gp.tensor_copy(f1_hi[:], f1raw[:])
            gp.tensor_copy(f2_hi[:], f2raw[:])
            gp.drain()
            gp.tensor_tensor(f1_lo[:], f1raw[:], f1_hi[:].bitcast(F32), ALU.subtract)
            gp.tensor_tensor(f2_lo[:], f2raw[:], f2_hi[:].bitcast(F32), ALU.subtract).then_inc(s["f_ready"], 1)

        @block.tensor
        def _(pe):
            def products(out, terms, halves):
                every = [(a(c), b(c)) for c in range(halves) for a, b in terms]
                for n, (a, b) in enumerate(every):
                    last = pe.matmul(out, a, b, start=n == 0, stop=n == len(every) - 1)
                return last

            def norm(t, g):
                pe.wait_ge(LV.sem, LV.at(t, f"xn {g}"))
                for c in range(C):
                    for j in range(GJ):
                        last = pe.transpose(ps[:, 2 * g + c, j * P:(j + 1) * P], xn[:, g * GJ + j, c * P:(c + 1) * P], eye[:])
                last.then_inc(LP.sem, LP.one(f"turned {g}"))

            def attention(att):
                def acts(part, g, width=GT, at=0):
                    return lambda c: part[:, c, g * GT + at:g * GT + at + width]

                def turn_probs(i, j):
                    pe.wait_ge(s["probs_made"], unit(att, i, j))
                    for p in range(2):
                        last = pe.transpose(ps[:, BQ, p * P:(p + 1) * P], probs[:, 2 * p:2 * p + 2, :], eye[:])
                    last.then_inc(s["probs_turned"], 1)

                def heads_out(i, j):
                    pp, g, hd = parts(j)
                    pe.wait_ge(s["pT_read"], unit(att, i, j))
                    pe.wait_ge(s["v_read"], unit(att, i, j + 1 - hd))
                    ctx = ps[:, BC, :].rearrange("p (q s r l) -> p q r s l", q=2, s=2, r=2)
                    for p in range(2):
                        for r in range(2):
                            last = pe.matmul(ctx[:, p, r], v[:, g % 2, 2 * p + r, hd * K3:(hd + 1) * K3],
                                             pT[:, 2 * p + r, :], start=True, stop=True)
                    last.then_inc(s["ctx_made"], 1)

                def project_out(i, j, first):
                    pp, g, hd = parts(j)
                    pe.wait_ge(s["ctx_lo_made"], unit(att, i, j))
                    if hd == 0 and not first:
                        pe.wait_ge(s["out_added"], added(att, i, j - 1))
                    for t in range(GJ):
                        for n, (a, b) in enumerate(passes(c_hi, c_lo, w_hi, w_lo)):
                            last = pe.matmul(ps[:, BO + t // 2, (t % 2) * E:(t % 2 + 1) * E], a[:, t * P:(t + 1) * P],
                                             b[:, pp, WO + hd * E:WO + (hd + 1) * E], start=hd == 0 and n == 0 and t % 2 == 0,
                                             stop=hd == 1 and n == 2, skip_group_check=True)
                    last.then_inc(s["out_made"], 1)

                def slots(i, peeled, last_turn):
                    for j in range(SLOTS):
                        pp, g, hd = parts(j)

                        def weights(part, at, width=K3):
                            return lambda c: part[:, pp, at + c * width:at + (c + 1) * width]

                        before = not (peeled and j == 0)
                        if j % PSLOTS == 0:
                            pe.wait_ge(s["w_ready"], i * 2 + (att * PAIRS + pp + 1))
                        if peeled and pp == 0 and hd == 0:
                            pe.wait_ge(LV.sem, LV.at(att, f"split {g}"))
                        if peeled and j == 1:
                            norm(att, 3)
                        products(ps[:, BQ, :], [(weights(a, WQ + hd * C * K3), acts(b, g))
                                                for a, b in passes(w_hi, w_lo, h_hi, h_lo)], C).then_inc(s["q_made"], 1)
                        if before:
                            pe.wait_ge(s["k_read"], unit(att, i, j - 1))
                        products(ps[:, BK, :], [(weights(a, WK + hd * C * K3), acts(b, g))
                                                for a, b in passes(w_hi, w_lo, ctx_hi, ctx_lo)], C).then_inc(s["k_made"], 1)
                        if peeled and j == 2:
                            pe.wait_ge(LA.sem, LA.at(att, "hT 3"))
                        if not (peeled and j < 2):
                            project_out(i, j - 2, peeled and j == 2)
                        pe.wait_ge(s["q_read"], unit(att, i, j))
                        if before:
                            turn_probs(i, j - 1)
                            pe.wait_ge(s["v_read"], unit(att, i, j - 1))
                        if peeled and j == 0:
                            pe.wait_ge(LA.sem, LA.at(att, "hT 2"))
                        for t in range(2):
                            last = products(ps[:, BV, t * 2 * K3:(t + 1) * 2 * K3],
                                            [(acts(a, g, P, (2 * hd + t) * P), weights(b, WV, 2 * K3))
                                             for a, b in passes(ctx_hi, ctx_lo, w_hi, w_lo)], C)
                        last.then_inc(s["v_made"], 1)
                        pe.wait_ge(s["k_read"], unit(att, i, j))
                        if before:
                            pe.wait_ge(s["less_made"], unit(att, i, j - 1))
                        for t in range(GJ):
                            place = t // 2 * 4 + t % 2
                            last = pe.matmul(ps[:, BS + t // 2, t % 2 * SW:t % 2 * SW + 2 * (L + 1)], qT[:, t * P:(t + 1) * P],
                                             kT[:, hd, place:place + 3:2, :], start=True, stop=True)
                        last.then_inc(s["scores_made"], 1)
                        if before:
                            heads_out(i, j - 1)

                turns(pe, slots)
                i, j = ITER - 1, SLOTS - 1
                project_out(i, j - 1, False)
                turn_probs(i, j)
                heads_out(i, j)
                project_out(i, j, False)

            for att in range(2):
                for g in range(GROUPS - 1):
                    norm(att, g)
                attention(att)
            for g in range(GROUPS - 1):
                norm(2, g)
            pe.wait_ge(s["f_ready"], 1)
            for g in range(GROUPS):
                pe.wait_ge(LV.sem, LV.at(2, f"split {g}"))
                for n in range(FT + 1):
                    m = g * FT + n
                    if n < FT:
                        if m >= 2:
                            pe.wait_ge(s["gelu_made"], m - 1)
                        terms = [(lambda c, a=a: a[:, c, n * P:(n + 1) * P], lambda c, b=b: b[:, c, g * GT:(g + 1) * GT])
                                 for a, b in passes(f1_hi, f1_lo, h_hi, h_lo)]
                        products(ps[:, n % 2, :], terms, C).then_inc(s["fc1_made"], 1)
                    if g == 0 and n == 1:
                        norm(2, 3)
                        pe.wait_ge(LA.sem, LA.at(2, "hT 3"))
                    if n:
                        f = n - 1
                        pe.wait_ge(s["gelu_split"], g * FT + f + 1)
                        if f == 0 and g:
                            pe.wait_ge(s["fc2_added"], g)
                        for t in range(GJ):
                            three = passes(g_hi, g_lo, f2_hi, f2_lo)
                            for o, (a, b) in enumerate(three):
                                last = pe.matmul(ps[:, 4 + t, 0:E], a[:, f % 2, t * P:(t + 1) * P], b[:, f, :],
                                                 start=f == 0 and o == 0, stop=f == FT - 1 and o == 2)
                        last.then_inc(s["fc2_made"], 1)

        @block.scalar
        def _(act):
            def deviation(t, g):
                if t:
                    act.wait_ge(s["stats_made"], (t - 1) * GROUPS + g + 1)
                act.activation(sd[:, tiles(g)], mv[:, tiles(g), 1], ACT.Sqrt, bias=eps[:]).then_inc(LA.sem, LA.one(f"sd {g}"))

            def affine(t, g):
                act.wait_ge(LP.sem, LP.at(t, f"turned {g}"))
                for c in range(C):
                    last = act.activation(turned(g)[:, c, :], ps[:, 2 * g + c, :], ACT.Identity,
                                          bias=vec(f"o{t + 1}", c), scale=vec(f"s{t + 1}", c))
                last.then_inc(LA.sem, LA.one(f"hT {g}"))

            def attention(att):
                def probs_out(i, j):
                    act.wait_ge(s["probs_turned"], unit(att, i, j))
                    for h in range(2):
                        o = slice(h * L, (h + 1) * L)
                        last = act.copy(pT[o, :, o], ps[o, BQ, 0:2 * P].rearrange("p (n q) -> p n q", n=GJ))
                    last.then_inc(s["pT_read"], 1)

                def ctx_out(i, j):
                    pp, g, hd = parts(j)
                    act.wait_ge(s["ctx_made"], unit(att, i, j))
                    act.activation(c_hi[:], ps[:, BC, :], ACT.Identity, bias=hb[:, pp, 3, hd:hd + 1]).then_inc(s["ctx_hi_made"], 1)

                def slots(i, peeled, last_turn):
                    for j in range(SLOTS):
                        pp, g, hd = parts(j)
                        if j % PSLOTS == 0:
                            for m, name in enumerate(("bq", "bk", "bias_k", "bias_v")):
                                act.copy(hb[:, pp, m, :], col[:, bass.ds(i * 4 + (H0[name, att] + 2 * pp), 2)])
                            act.drain()
                        act.wait_ge(s["q_made"], unit(att, i, j))
                        act.activation(qT[:], ps[:, BQ, :], ACT.Identity, bias=hb[:, pp, 0, hd:hd + 1]).then_inc(s["q_read"], 1)
                        act.wait_ge(s["k_made"], unit(att, i, j))
                        if g == 0:
                            act.copy(kT[:, hd, :, L:L + 1], hb[:, pp, 2, hd:hd + 1].unsqueeze(1).broadcast_to([P, GB, 1]))
                        act.activation(kT[:, hd, :, 0:L], ps[:, BK, :].rearrange("p (b l) -> p b l", b=GB), ACT.Identity,
                                       bias=hb[:, pp, 1, hd:hd + 1]).then_inc(s["k_read"], 1)
                        if peeled and j == 1:
                            affine(att, 3)
                        if not (peeled and j == 0):
                            probs_out(i, j - 1)
                            if last_turn and pp and j % 2 == 0 and g >= 2:
                                deviation(att + 1, g - 2)
                            ctx_out(i, j - 1)
                        act.wait_ge(s["less_made"], unit(att, i, j))
                        act.activation(e[:], e[:], ACT.Exp, scale=float(K3) ** -0.5).then_inc(s["exp_made"], 1)

                turns(act, slots)
                probs_out(ITER - 1, SLOTS - 1)
                ctx_out(ITER - 1, SLOTS - 1)
                deviation(att + 1, 2)
                deviation(att + 1, 3)
                for g in range(GROUPS - 1):
                    affine(att + 1, g)

            for g in range(GROUPS):
                deviation(0, g)
            act.copy(w_hi[:, 0, :], wraw[:]).then_inc(s["first_hi_made"], 1)
            for g in range(GROUPS - 1):
                affine(0, g)
            act.wait_ge(s["blocks_clear"], 1)
            for att in range(2):
                attention(att)
            for m in range(GROUPS * FT):
                act.wait_ge(s["fc1_made"], m + 1)
                if m >= 2:
                    act.wait_ge(s["gelu_split"], m - 1)
                act.activation(ge[:, m % 2, :], ps[:, m % 2, :], ACT.Gelu, bias=col[:, FC0 + m % FT:FC0 + m % FT + 1])\
                    .then_inc(s["gelu_made"], 1)
                if m == 1:
                    affine(2, 3)

        @block.vector
        def _(ve):
            def stats(t, g):
                for j in range(g * GJ, (g + 1) * GJ):
                    ve.bn_stats(st[:, j, :], xres[:, j, :])
                ve.drain()
                for j in range(g * GJ, (g + 1) * GJ):
                    last = ve.bn_aggr(mv[:, j, :], st[:, j, :])
                last.then_inc(s["stats_made"], 1)

            def normalise(t, g):
                ve.wait_ge(LA.sem, LA.at(t, f"sd {g}"))
                ve.reciprocal(rs[:, tiles(g)], sd[:, tiles(g)])
                ve.drain()
                if t == 2 and g == 0:
                    ve.wait_ge(s["f_ready"], 1)
                for j in range(g * GJ, (g + 1) * GJ):
                    last = ve.tensor_scalar(xn[:, j, :], xres[:, j, :], mv[:, j, 0:1], rs[:, j:j + 1], ALU.subtract, ALU.mult)
                last.then_inc(LV.sem, LV.one(f"xn {g}"))

            def split(t, g):
                ve.wait_ge(LA.sem, LA.at(t, f"hT {g}"))
                hi, lo = h_hi[:, :, g * GT:(g + 1) * GT], h_lo[:, :, g * GT:(g + 1) * GT]
                ve.tensor_copy(hi, turned(g))
                ve.drain()
                ve.tensor_tensor(lo, turned(g), hi.bitcast(F32), ALU.subtract).then_inc(LV.sem, LV.one(f"split {g}"))

            def after(t, n):
                ve.tensor_tensor(xres[:, tiles(n), :], xres[:, tiles(n), :], brow[:, t:t + 1, :].broadcast_to([P, GJ, E]), ALU.add)
                if n + 1 < GROUPS:
                    split(t, n + 1)

            def attention(att):
                def ctx_lo_part(i, j):
                    pp, g, hd = parts(j)
                    ve.wait_ge(s["ctx_hi_made"], unit(att, i, j))
                    ve.scalar_tensor_tensor(c_lo[:], ps[:, BC, :], hb[:, pp, 3, hd:hd + 1], c_hi[:].bitcast(F32),
                                            ALU.add, ALU.subtract).then_inc(s["ctx_lo_made"], 1)

                def add_out(i, j):
                    pp, g, hd = parts(j)
                    ve.wait_ge(s["out_made"], unit(att, i, j))
                    ve.tensor_tensor(xres[:, tiles(g), :], ps[:, BO:BO + 2, :].rearrange("p a (b x) -> p (a b) x", x=E),
                                     xres[:, tiles(g), :], ALU.add).then_inc(s["out_added"], 1)

                def slots(i, peeled, last_turn):
                    for j in range(SLOTS):
                        pp, g, hd = parts(j)
                        if hd and not (peeled and j < 3):
                            add_out(i, j - 2)
                        ve.wait_ge(s["v_made"], unit(att, i, j))
                        if j % PSLOTS == 0:
                            ve.wait_ge(s["w_ready"], i * 2 + (att * PAIRS + pp + 1))
                        ve.tensor_tensor(v[:, g % 2, 2 * hd:2 * hd + 2], ps[:, BV, :].rearrange("p (t x) -> p t x", t=2),
                                         vb[:, pp:pp + 1, :].broadcast_to([P, 2, 2 * K3]), ALU.add).then_inc(s["v_read"], 1)
                        ve.wait_ge(s["scores_made"], unit(att, i, j))
                        own = []
                        for h in range(2):
                            o = slice(h * L, (h + 1) * L)
                            sc3 = ps[o, BS:BS + 2, :].rearrange("p a (b x) -> p (a b) x", x=SW)[:, :, h * (L + 1):(h + 1) * (L + 1)]
                            own.append((o, sc3))
                            ve.tensor_reduce(r3[o, 0, :], sc3, AX, ALU.max)
                        ve.drain()
                        for o, sc3 in own:
                            last = ve.tensor_tensor(e[o], sc3, r3[o, 0, :].unsqueeze(2).broadcast_to([L, GJ, L + 1]), ALU.subtract)
                        last.then_inc(s["less_made"], 1)
                        if not (peeled and j == 0):
                            ctx_lo_part(i, j - 1)
                        ve.wait_ge(s["exp_made"], unit(att, i, j))
                        ve.tensor_reduce(r3[:, 1, :], e[:], AX, ALU.add)
                        ve.drain()
                        ve.reciprocal(r3[:, 2, :], r3[:, 1, :])
                        ve.drain()
                        ve.tensor_tensor(probs[:], e[:, :, 0:L], r3[:, 2, :].unsqueeze(2).broadcast_to([P, GJ, L]), ALU.mult)\
                            .then_inc(s["probs_made"], 1)
                        if peeled and j < GROUPS:
                            after(att, j)
                        if last_turn and pp and g:
                            if hd:
                                stats(att + 1, g - 1)
                            elif g >= 2:
                                normalise(att + 1, g - 2)

                turns(ve, slots)
                ctx_lo_part(ITER - 1, SLOTS - 1)
                normalise(att + 1, 2)
                add_out(ITER - 1, SLOTS - 1)
                ve.drain()
                stats(att + 1, 3)
                split(att + 1, 0)
                normalise(att + 1, 3)

            for g in range(GROUPS - 1):
                normalise(0, g)
            split(0, 0)
            normalise(0, 3)
            for att in range(2):
                attention(att)
            for g in range(GROUPS):
                for f in range(FT):
                    m = g * FT + f
                    ve.wait_ge(s["gelu_made"], m + 1)
                    if m >= 2:
                        ve.wait_ge(s["fc2_made"], m - 1)
                    ve.tensor_copy(g_hi[:, m % 2, :], ge[:, m % 2, :])
                    ve.drain()
                    ve.tensor_tensor(g_lo[:, m % 2, :], ge[:, m % 2, :], g_hi[:, m % 2, :].bitcast(F32), ALU.subtract)\
                        .then_inc(s["gelu_split"], 1)
                    if m < GROUPS:
                        after(2, m)
                ve.wait_ge(s["fc2_made"], (g + 1) * FT)
                ve.tensor_tensor(xres[:, tiles(g), :], ps[:, 4:8, 0:E], xres[:, tiles(g), :], ALU.add).then_inc(s["fc2_added"], 1)


def _halves(v):
    return v.reshape(C, P).T


def _kxm(w):
    return w.reshape(-1, P, w.shape[-1]).transpose(1, 0, 2)


def kernel(**a):
    import concourse.bacc as bacc
    from concourse.bass_utils import run_bass_kernel_spmd

    a = {n: np.asarray(v) for n, v in a.items()}
    l0, l1, l2, l3 = ({n[len(p):]: v for n, v in a.items() if n.startswith(p)}
                      for p in ("L0_xattn_", "L1_xattn_", "L2_xattn_", "L3_xattn_"))
    f32 = np.float32
    vectors = {n: l0[n] for n in ("ln1_w", "ln1_b", "ln2_w", "ln2_b", "maa_x", "time_decay", "gn_w", "gn_b",
                                  "ffn_maa_k", "ffn_maa_r")}
    vectors |= {f"stack{i}": l0["maa_stack"][i] for i in range(MIX)}
    vectors |= {"faaaa": l0["faaaa"].reshape(E), "ln_gamma": l1["ln_gamma"], "ln_beta": l1["ln_beta"]}
    vectors |= {"s1": l3["ln1_scale"], "o1": l3["ln1_offset"], "s2": l3["ln2_scale"], "o2": l3["ln2_offset"],
                "s3": l3["ln_mlp_scale"], "o3": l3["ln_mlp_offset"]}
    columns = [_halves(vectors[n]) for n in VECS]
    for at in ("1", "2"):
        columns += [l3[n + at].reshape(H3, K3).T for n in ("bq", "bk", "bias_k", "bias_v")]
    columns.append(l3["b_fc1"].reshape(FT, P).T)
    columns += [np.tile(l2[n], 2).reshape(P, 1) for n in ("bn", "bm", "bl", "bo")]
    even = (np.arange(P) // D1 % 2 == 0).astype(f32)
    columns += [even.reshape(P, 1), 1 - even.reshape(P, 1), np.broadcast_to(l1["gate"].reshape(1, 1), (P, 1))]
    cols = np.concatenate(columns, axis=1)

    square = [l0["Wr"].T, l0["Wk"].T, l0["Wv"].T, l0["Wg"].T, l0["Wo"].T, l0["ffn_Wk"].T, l0["ffn_Wr"].T,
              l0["ffn_Wv"].T, l1["Wq"].T, l1["Wk"].T, l1["Wv"].T, l1["Wo"].T]
    sq = np.stack([_kxm(w) for w in square], axis=1)
    n = np.arange(P)
    head = n[:, None] // S == n[None, :] // S
    spread = np.stack([head & (n[:, None] % S == d) for d in range(S)], axis=1).astype(f32)
    sel = np.stack([spread, spread.transpose(2, 1, 0)], axis=1)
    blocks = np.stack([head.astype(f32), head.astype(f32) / f32(S)], axis=1)
    w2l = np.zeros((P, 4, P), f32)
    for i, name in enumerate(("Wn", "Wm", "Wl", "Wo")):
        for o in (0, L):
            w2l[o:o + L, i, o:o + L] = l2[name].T
    pairs = []
    for at in ("1", "2"):
        qk = [_kxm(l3[w + at]).reshape(P, C, H3 // 2, 2, K3).transpose(2, 0, 3, 1, 4) for w in ("wq", "wk")]
        vv = _kxm(l3["wv" + at]).reshape(P, C, H3 // 2, 2 * K3).transpose(2, 0, 1, 3)
        oo = l3["wo" + at].reshape(H3 // 2, 2, K3, E).transpose(0, 2, 1, 3)
        pairs.append(np.concatenate([t.reshape(H3 // 2, P, -1) for t in (*qk, vv, oo)], axis=2))
    w3 = np.concatenate(pairs)
    vrows = np.concatenate([np.stack([l3[n + at].reshape(H3 // 2, 2 * K3) for n in ("bv", "bias_v")], axis=1)
                            for at in ("1", "2")])
    arrays = {
        "x": a["x"], "ctx": a["ctx_2048"], "mask": a["mask_BxS2_bf1"].view(np.uint8), "cols": cols, "sq": sq,
        "maa_w1": _kxm(l0["maa_w1"]), "maa_w2": l0["maa_w2"].reshape(MIX * LORA, E),
        "dec_w1": _kxm(l0["decay_w1"]), "dec_w2": l0["decay_w2"], "sel": sel, "blocks": blocks, "w2l": w2l,
        "rows3": np.stack([l3["bo1"], l3["bo2"], l3["b_fc2"]]), "w3": w3, "vrows": vrows,
        "fc1": _kxm(l3["w_fc1"]), "fc2": _kxm(l3["w_fc2"]), "ident": np.eye(P, dtype=f32),
    }
    nc = bacc.Bacc("TRN2", target_bir_lowering=False, num_devices=1)
    ins, handles = {}, {}
    for name, v in arrays.items():
        ins[f"in_{name}"] = np.ascontiguousarray(v)
        handles[name] = nc.dram_tensor(f"in_{name}", v.shape, mybir.dt.from_np(v.dtype), kind="ExternalInput").ap()
    handles["out"] = nc.dram_tensor("out_0", (B, L, E), F32, kind="ExternalOutput").ap()
    program(nc, **handles)
    r = run_bass_kernel_spmd(nc, [ins], core_ids=[0])
    return r.results[0]["out_0"]
```
